# Optimizing a Trainium2 kernel written in Bass

```python
import numpy as np
import jax
import jax.numpy as jnp

def _softmax(x, axis=-1):
    return jax.nn.softmax(x, axis=axis)

def _gelu(x):
    return jax.nn.gelu(x, approximate=True)

def _silu(x):
    return jax.nn.silu(x)

def _sigmoid(x):
    return jax.nn.sigmoid(x)

def _layernorm(x, axis=-1, eps=1e-05):
    m = jnp.mean(x, axis=axis, keepdims=True)
    v = jnp.var(x, axis=axis, keepdims=True)
    return (x - m) / jnp.sqrt(v + eps)

def _scatter_add(tgt, idx, src, axis=0):
    return tgt.at[idx].add(src)

def _segment_sum(src, seg, n):
    return jax.ops.segment_sum(src, seg, n)
kernel_name = 'mk_decoder_postln_d1_seqx_r8_f606eb'

def setup_inputs(seed: int=0):
    np.random.seed(seed)
    _w = jnp.asarray

    def _rec_inputs():
        import jax
        import jax.numpy as jnp
        _rk = jax.random.key(seed)
        x = -0.000125 + 0.9999 * jax.random.normal(jax.random.fold_in(_rk, 1), (1, 1024, 128), jnp.float32)
        _lenS = 1024 - jax.random.randint(jax.random.fold_in(_rk, 7), (1,), 0, max(1, 1024 // 4) + 1, jnp.int32)
        _lenS2 = 6404 - jax.random.randint(jax.random.fold_in(_rk, 8), (1,), 0, max(1, 6404 // 4) + 1, jnp.int32)
        _ctx_1024P = jax.random.normal(jax.random.fold_in(_rk, 11), (1, 16, 128), jnp.float32)
        _ctx_1024c = jax.random.dirichlet(jax.random.fold_in(_rk, 511), 0.3 * jnp.ones((16,), jnp.float32), (1, 6404))
        _ctx_1024t = jnp.einsum('bsk,bkd->bsd', _ctx_1024c, _ctx_1024P)
        _ctx_1024t = _ctx_1024t * jax.lax.rsqrt(jnp.mean(jnp.square(_ctx_1024t)) + 1e-12) * 0.953939
        ctx_1024 = -1.78809e-06 + 0.0312453 * (_ctx_1024t + 0.3 * jax.random.normal(jax.random.fold_in(_rk, 611), (1, 6404, 128), jnp.float32))
        return (x, ctx_1024)
    x, ctx_1024 = _rec_inputs()

    def _L0_attn_setup():
        import jax, jax.numpy as jnp
        import numpy as np
        B, N, C = (2, 256, 128)
        H = 16
        D = C // H
        key = jax.random.key(seed)
        ks = jax.random.split(key, 5)
        s = 0.02
        return {'x': jax.random.normal(ks[0], (B, N, C), dtype=jnp.float32), 'qkv_w': jax.random.normal(ks[1], (C, 3 * C), dtype=jnp.float32) * s, 'qkv_b': jax.random.normal(ks[2], (3 * C,), dtype=jnp.float32) * s, 'proj_w': jax.random.normal(ks[3], (C, C), dtype=jnp.float32) * s, 'proj_b': jax.random.normal(ks[4], (C,), dtype=jnp.float32) * s}
    _L0_attn_all = _L0_attn_setup()
    _L0_attn_in = {k: v for k, v in _L0_attn_all.items() if k in ('qkv_w', 'qkv_b', 'proj_w', 'proj_b')}
    del _L0_attn_all

    def _L0_xattn_setup():
        import jax, jax.numpy as jnp
        import numpy as np
        E, T, H, F = (16, 256, 128, 512)
        key = jax.random.key(seed)
        kx, k1, k2, k3 = jax.random.split(key, 4)
        s = 1.0 / np.sqrt(H)
        return {'x': jax.random.normal(kx, (E, T, H), dtype=jnp.float32), 'w1': jax.random.normal(k1, (E, F, H), dtype=jnp.float32) * s, 'v1': jax.random.normal(k2, (E, F, H), dtype=jnp.float32) * s, 'w2': jax.random.normal(k3, (E, F, H), dtype=jnp.float32) * s}
    _L0_xattn_all = _L0_xattn_setup()
    _L0_xattn_in = {k: v for k, v in _L0_xattn_all.items() if k in ()}
    del _L0_xattn_all

    def _L0_ffn_setup():
        import jax, jax.numpy as jnp
        import numpy as np
        N_EXPERTS = 8
        N_GROUP = 4
        TOPK_GROUP = 2
        TOP_K = 2
        HIDDEN = 128
        INTER = 256
        B, S = (1, 128)

        def _grouped_topk(scores):
            T, E = scores.shape
            per_group = E // N_GROUP
            group_scores = scores.reshape(T, N_GROUP, per_group).max(-1)
            _, gidx = jax.lax.top_k(group_scores, TOPK_GROUP)
            gmask = jnp.zeros((T, N_GROUP), scores.dtype).at[jnp.arange(T)[:, None], gidx].set(1.0)
            smask = jnp.repeat(gmask, per_group, axis=1)
            masked = jnp.where(smask > 0, scores, 0.0)
            topk_w, topk_ids = jax.lax.top_k(masked, TOP_K)
            topk_w = topk_w / topk_w.sum(-1, keepdims=True)
            return (topk_ids, topk_w)
        key = jax.random.key(seed)
        k1, k2, k3, k4 = jax.random.split(key, 4)
        return {'hidden_states': jax.random.normal(k1, (B, S, HIDDEN), jnp.float32), 'gate_w': jax.random.normal(k2, (N_EXPERTS, HIDDEN), jnp.float32) * 0.02, 'w13_weight': jax.random.normal(k3, (N_EXPERTS, 2 * INTER, HIDDEN), jnp.float32) * 0.02, 'w2_weight': jax.random.normal(k4, (N_EXPERTS, HIDDEN, INTER), jnp.float32) * 0.02}
    _L0_ffn_all = _L0_ffn_setup()
    _L0_ffn_in = {k: v for k, v in _L0_ffn_all.items() if k in ('gate_w', 'w13_weight', 'w2_weight')}
    del _L0_ffn_all
    return {'x': x, 'ctx_1024': ctx_1024, 'L0_attn_qkv_w': _L0_attn_in['qkv_w'], 'L0_attn_qkv_b': _L0_attn_in['qkv_b'], 'L0_attn_proj_w': _L0_attn_in['proj_w'], 'L0_attn_proj_b': _L0_attn_in['proj_b'], 'L0_ffn_gate_w': _L0_ffn_in['gate_w'], 'L0_ffn_w13_weight': _L0_ffn_in['w13_weight'], 'L0_ffn_w2_weight': _L0_ffn_in['w2_weight']}

def reference(x, ctx_1024, L0_attn_qkv_w, L0_attn_qkv_b, L0_attn_proj_w, L0_attn_proj_b, L0_ffn_gate_w, L0_ffn_w13_weight, L0_ffn_w2_weight):
    import jax
    import jax.numpy as jnp

    def _L0_attn_ref(x, qkv_w, qkv_b, proj_w, proj_b):
        import jax, jax.numpy as jnp
        import numpy as np
        B, N, C = (2, 256, 128)
        H = 16
        D = C // H
        b, n, c = x.shape
        scale = (c // H) ** (-0.5)
        qkv = x @ qkv_w + qkv_b
        qkv = qkv.reshape(b, n, 3, H, D)
        q, k, v = jnp.moveaxis(qkv, 2, 0)
        attn = jnp.einsum('bnhd,bmhd->bhnm', q, k) * scale
        attn = jax.nn.softmax(attn, axis=-1)
        out = jnp.einsum('bhnm,bmhd->bnhd', attn, v).reshape(b, n, c)
        out = out @ proj_w + proj_b
        return out

    def _L0_xattn_ref(x, w1, v1, w2):
        import jax, jax.numpy as jnp
        import numpy as np
        E, T, H, F = (16, 256, 128, 512)
        x1 = jnp.einsum('eth,efh->etf', x, w1)
        x2 = jnp.einsum('eth,efh->etf', x, v1)
        h = jax.nn.gelu(x1, approximate=True) * x2
        return jnp.einsum('etf,efh->eth', h, w2)

    def _L0_ffn_ref(hidden_states, gate_w, w13_weight, w2_weight):
        import jax, jax.numpy as jnp
        import numpy as np
        N_EXPERTS = 8
        N_GROUP = 4
        TOPK_GROUP = 2
        TOP_K = 2
        HIDDEN = 128
        INTER = 256
        B, S = (1, 128)

        def _grouped_topk(scores):
            T, E = scores.shape
            per_group = E // N_GROUP
            group_scores = scores.reshape(T, N_GROUP, per_group).max(-1)
            _, gidx = jax.lax.top_k(group_scores, TOPK_GROUP)
            gmask = jnp.zeros((T, N_GROUP), scores.dtype).at[jnp.arange(T)[:, None], gidx].set(1.0)
            smask = jnp.repeat(gmask, per_group, axis=1)
            masked = jnp.where(smask > 0, scores, 0.0)
            topk_w, topk_ids = jax.lax.top_k(masked, TOP_K)
            topk_w = topk_w / topk_w.sum(-1, keepdims=True)
            return (topk_ids, topk_w)
        Bm, Sm, H = hidden_states.shape
        x = hidden_states.reshape(-1, H)
        T = x.shape[0]
        scores = jax.nn.softmax(x @ gate_w.T, axis=-1)
        topk_ids, topk_w = _grouped_topk(scores)
        combine = jnp.zeros((T, N_EXPERTS), x.dtype).at[jnp.arange(T)[:, None], topk_ids].add(topk_w)
        gu = jnp.einsum('th,eih->tei', x, w13_weight)
        gate, up = (gu[..., :INTER], gu[..., INTER:])
        act = jax.nn.silu(gate) * up
        act = act * combine[:, :, None]
        out = jnp.einsum('tei,ehi->th', act, w2_weight)
        return out.reshape(Bm, Sm, H)
    x = _layernorm(x + _L0_attn_ref(x, L0_attn_qkv_w, L0_attn_qkv_b, L0_attn_proj_w, L0_attn_proj_b), axis=-1)
    x = _layernorm(x + _L0_xattn_ref(x, ctx_1024, ctx_1024, ctx_1024), axis=-1)
    x = _layernorm(x + _L0_ffn_ref(x, L0_ffn_gate_w, L0_ffn_w13_weight, L0_ffn_w2_weight), axis=-1)
    return x

_drawn_inputs = setup_inputs


def setup_inputs(seed=0):
    import zlib

    import numpy as np

    out = dict(_drawn_inputs(seed))
    spreads = {}
    factors = {'L0_attn_qkv_w': 8.0,
     'L0_attn_qkv_b': 8.0,
     'L0_attn_proj_w': 8.0,
     'L0_attn_proj_b': 4.418,
     'L0_ffn_gate_w': 8.0,
     'L0_ffn_w13_weight': 8.0,
     'L0_ffn_w2_weight': 8.0}
    for name, (base, spread) in spreads.items():
        noise = np.random.default_rng([zlib.crc32(name.encode()), seed]).standard_normal(out[name].shape)
        drawn = base * np.exp(spread * noise) if base else spread * noise
        out[name] = jnp.asarray(drawn.astype(out[name].dtype))
    for name, factor in factors.items():
        out[name] = (out[name] * factor).astype(out[name].dtype)
    return out
```

```python
import concourse.bass as bass
from concourse import mybir
from contextlib import ExitStack


P = 128
N = 1024
C = 128
H = 16
D = C // H
F = 6404
NE = 8
INTER = 256
TB = N // P
HALF = N // 2
HB = TB // 2
EPS = 1e-5
SCALE = float(D) ** -0.5

PARTS = 3
PAIRS = PARTS * D
MROW = PARTS * PAIRS
ONES = 0x3F803F80
GH = 4
NG = H // GH
VW = 32
KB = N // P
UNITS = 2 * NG
STEPS = UNITS * KB
UT = GH * HB
LEAD = 4
MAX_TILES = UNITS * UT

FB = F // P
FR = F - FB * P
CTX_CHUNKS = -(-(FB + 1) // 4)
CTX_LOADS = 5
XJ = FB + 1
XA = 2 * XJ
LAG = 2
WT_CHUNKS = NE + NE // 2

PROJ = (35, 3)
ACC = XJ + LAG
WT_FIRST, WT_EVERY = 18, 4


def max_tiles_at(n):
    first = UT + LEAD + 2 * n
    return range(min(first, MAX_TILES), min(first + 2, MAX_TILES))


def max_tile_of(t):
    u, i = divmod(t, UT)
    half, g = divmod(u, NG)
    return u, GH * g + i // HB, HB * half + i % HB


def context_chunk(c):
    blocks = range(4 * c, min(4 * c + 4, FB + 1))
    return blocks, 4 * c * P, min(4 * P, F - 4 * c * P)


def weight_chunk_at(k):
    w = (k - WT_FIRST) // WT_EVERY
    return w if k >= WT_FIRST and (k - WT_FIRST) % WT_EVERY == 0 and w < WT_CHUNKS else None


def build(nc, x, ctx, qkv_w, qkv_b, proj_w, proj_b, gate_w, w13, w2, out, kept_k, kept_q):
    f32 = mybir.dt.float32
    f32r = mybir.dt.float32r
    bf16 = mybir.dt.bfloat16
    u32 = mybir.dt.uint32
    i32 = mybir.dt.int32
    ALU = mybir.AluOpType
    ACT = mybir.ActivationFunctionType
    AX = mybir.AxisListType

    stack = ExitStack()
    with stack:
        def sb(name, shape, dt, scope=stack):
            return scope.enter_context(nc.sbuf_tensor(name, shape, dt))

        def sem(name):
            return stack.enter_context(nc.semaphore(name))

        ident = sb("ident", [P, P], f32)
        x_rows = sb("x_rows", [P, TB, C], f32)
        pre_norm = sb("pre_norm", [P, TB, C], f32)
        gate_T = sb("gate_T", [P, NE], f32)
        lt4 = sb("lt4", [P, 4, 4], f32)
        lt8 = sb("lt8", [P, NE, NE], f32)
        stats = sb("stats", [P, HB, 6], f32)
        mean_var = sb("mean_var", [P, HB, 2], f32)
        norm_s = sb("norm_s", [P, 4, HB], f32)
        ctx_rows = sb("ctx_rows", [P, FB, C], f32)
        ctx_rest = sb("ctx_rest", [FR, C], f32)
        ctx_T_hi = sb("ctx_T_hi", [P, F], f32r)
        ctx_T_lo = sb("ctx_T_lo", [P, F], f32r)
        stage = sb("stage", [P, 2, 512], f32)
        x1a_T_hi = sb("x1a_T_hi", [P, HALF], f32r)
        x1a_T_lo = sb("x1a_T_lo", [P, HALF], f32r)

        att = ExitStack()
        q_stack = sb("q_stack", [P, 2, H, HALF], bf16, att)
        k_stack = sb("k_stack", [P, H, N], bf16, att)
        v_strip = sb("v_strip", [P, KB, H, VW], f32, att)
        att_rows = sb("att_rows", [P, TB, C], f32, att)
        att_T = sb("att_T", [P, HALF], f32, att)
        wqkv = sb("wqkv", [P, 3 * C], f32, att)
        bias_col = sb("bias_col", [P, 2], f32, att)
        bias_v = sb("bias_v", [P, C], f32, att)
        wproj = sb("wproj", [P, C], f32, att)
        bias_p = sb("bias_p", [P, C], f32, att)
        neg_max = sb("neg_max", [P, UNITS, UT], f32, att)
        m_parts = sb("m_parts", [UT, 2, PARTS, P], bf16, att)
        m_rest = sb("m_rest", [UT, 2, P], f32, att)
        recip = sb("recip", [P, 2, HB * GH], f32, att)
        pre = ExitStack()
        x_T = sb("x_T", [P, N], f32, pre)
        q_parts = sb("q_parts", [P, PARTS, N], bf16, pre)
        k_parts = sb("k_parts", [P, PARTS, N], bf16, pre)
        k_rest = sb("k_rest", [P, N], f32, pre)
        q_rest = att_rows[:, :, :].rearrange("p t c -> p (t c)")
        pre.close()
        probs = sb("probs", [P, 2, GH, HALF], f32, att)
        o_T = sb("o_T", [P, 2, HALF], f32, att)
        att.close()

        gelu = sb("gelu", [P, 3, HALF], f32)
        hid = sb("hid", [P, 3, HALF], f32)
        w13_T_hi = sb("w13_T_hi", [P, NE * 2 * INTER], f32r)
        w13_T_lo = sb("w13_T_lo", [P, NE * 2 * INTER], f32r)
        w2_T = sb("w2_T", [P, NE * 2 * C], f32)
        w2_rows = sb("w2_rows", [P, NE, INTER], f32)
        rows_only = ExitStack()
        w13_rows = sb("w13_rows", [P, 4 * NE, C], f32, rows_only)
        rows_only.close()
        silu = sb("silu", [P, 3, HALF], f32)
        act = sb("act", [P, 4, HALF], f32)
        router = sb("router", [P, 8, HB, NE], f32)
        pair = sb("pair", [P, 2, HB * NE * NE], f32)
        small = sb("small", [P, 4, HB], f32)
        logits = sb("logits", [P, HB, NE], f32)
        combine = sb("combine", [P, TB, NE], f32)
        x1b_T_hi = sb("x1b_T_hi", [P, HALF], f32r)
        x1b_T_lo = sb("x1b_T_lo", [P, HALF], f32r)
        acc_T = sb("acc_T", [P, 2, HALF], f32)
        x2_T = sb("x2_T", [P, 2, HALF], f32)
        x2_T_hi = sb("x2_T_hi", [P, 2, HALF], f32r)
        x2_T_lo = sb("x2_T_lo", [P, 2, HALF], f32r)
        x1_T_hi = (x1a_T_hi, x1b_T_hi)
        x1_T_lo = (x1a_T_lo, x1b_T_lo)

        psum = stack.enter_context(nc.psum_tensor("psum", [P, 8, 512], f32))

        def pair_of_banks(n):
            b = 2 * (n % 2)
            return psum[:, b:b + 2, :].rearrange("p b c -> p (b c)")

        def score_bank(n):
            return psum[:, 4 + n % 3, :]

        pv_bank = psum[:, 7, :]
        acc_banks = (psum[:, 7, :], psum[:, 3, :])
        weight_bank = psum[:, 1, :]
        gate_up_banks = (psum[:, 4:6, :], psum[:, 6:8, :])
        down_banks = (psum[:, 1, :], psum[:, 3, :])

        x_here = sem("x_here")
        wqkv_here = sem("wqkv_here")
        proj_here = sem("proj_here")
        ctx_here = [sem(f"ctx_here{n}") for n in range(CTX_LOADS)]
        ctx_rest_here = sem("ctx_rest_here")
        experts_here = sem("experts_here")
        ident_made = sem("ident_made")
        strips_set = sem("strips_set")
        masks_made = sem("masks_made")
        pre_bias = sem("pre_bias")
        stack_set = sem("stack_set")
        x_T_half = sem("x_T_half")
        k_made = sem("k_made")
        q_made = sem("q_made")
        k_kept = sem("k_kept")
        q_kept = [sem(f"q_kept{half}") for half in range(2)]
        stacked = [sem(f"stacked{n}") for n in range(3)]
        vec_ready = sem("vec_ready")
        vec_free = sem("vec_free")
        chain = sem("chain")
        pool_chain = sem("pool_chain")
        m_made = sem("m_made")
        m_rows = sem("m_rows")
        score_ready = sem("score_ready")
        score_done = sem("score_done")
        ctx_split = sem("ctx_split")
        pv_done = sem("pv_done")
        pv_taken = sem("pv_taken")
        o_read = sem("o_read")
        xa_ready = sem("xa_ready")
        xa_gelu = sem("xa_gelu")
        xa_hid = sem("xa_hid")
        xa_summed = sem("xa_summed")
        wt_ready = sem("wt_ready")
        wt_taken = sem("wt_taken")
        wt_split = sem("wt_split")
        acc_taken = sem("acc_taken")
        x2_split = sem("x2_split")
        shifted = sem("shifted")
        exp_ready = sem("exp_ready")
        gate_ready = sem("gate_ready")
        up_ready = sem("up_ready")
        moe_silu = sem("moe_silu")
        moe_act = sem("moe_act")
        down_ready = sem("down_ready")
        down_taken = sem("down_taken")
        normed = sem("normed")
        stored = sem("stored")

        block = stack.enter_context(nc.Block())

        @block.sync
        def _(sp):
            def stack_k(heads, n):
                sp.wait_ge(stack_set, 2 * n + 1)
                sp.wait_ge(k_kept, 16 * PARTS)
                for a in range(PARTS):
                    sp.dma_start(k_stack[PAIRS * a:PAIRS * (a + 1), heads, :],
                                 kept_k.rearrange("j d h t -> (j d) h t")[:, heads, :]).then_inc(stacked[n], 16)

            def stack_q(half, heads, n):
                sp.wait_ge(stack_set, 2 * n + 2 if n < 2 else 5)
                sp.wait_ge(q_kept[half], 16 * PARTS)
                for a in range(PARTS):
                    src = kept_q[half, a][:, heads, :].rearrange("d h t -> d (h t)")
                    src = src.unsqueeze(0).broadcast_to([PARTS] + list(src.shape))
                    sp.dma_start(q_stack[PAIRS * a:PAIRS * (a + 1), half, heads, :].rearrange("r h t -> r (h t)"),
                                 src).then_inc(stacked[n], 16)

            x_view = x[0].rearrange("(t p) c -> p t c", p=P)
            sp.dma_start(x_rows[:, :, :], x_view).then_inc(x_here, 16)
            sp.dma_start(wqkv[:, :], qkv_w).then_inc(wqkv_here, 16)
            sp.dma_start(bias_col[:, :], qkv_b[0:2 * C].rearrange("(j p) -> p j", p=P),
                         allow_slow_non_contiguous=True).then_inc(wqkv_here, 16)
            sp.dma_start(bias_v[:, :], qkv_b[2 * C:3 * C].partition_broadcast(P)).then_inc(wqkv_here, 16)
            ctx_view = ctx[0, 0:FB * P, :].rearrange("(p j) c -> p j c", j=FB)
            per = FB // CTX_LOADS
            for n in range(CTX_LOADS):
                if n == 2:
                    for part in range(PARTS):
                        sp.wait_ge(k_made, part + 1)
                        sp.dma_start(kept_k[part].rearrange("d h t -> h d t"), k_parts[:, part, :]).then_inc(k_kept, 16)
                        sp.wait_ge(q_made, part + 1)
                        sp.dma_start(kept_q[0, part].rearrange("d h t -> h d t"),
                                     q_parts[:, part, 0:HALF]).then_inc(q_kept[0], 16)
                    stack_k(slice(0, GH), 0)
                    stack_q(0, slice(0, GH), 0)
                sp.dma_start(ctx_rows[:, n * per:(n + 1) * per, :],
                             ctx_view[:, n * per:(n + 1) * per, :]).then_inc(ctx_here[n], 16)
            for part in range(PARTS):
                sp.dma_start(kept_q[1, part].rearrange("d h t -> h d t"),
                             q_parts[:, part, HALF:N]).then_inc(q_kept[1], 16)
            stack_k(slice(GH, H), 1)
            stack_q(0, slice(GH, H), 1)
            stack_q(1, slice(0, H), 2)
            sp.dma_start(ctx_rest[:, :], ctx[0, FB * P:F, :]).then_inc(ctx_rest_here, 16)
            sp.dma_start(wproj[:, :], proj_w).then_inc(proj_here, 16)
            sp.dma_start(bias_p[:, :], proj_b.partition_broadcast(P)).then_inc(proj_here, 16)
            sp.dma_start(gate_T[:, :], gate_w.rearrange("e c -> c e"), allow_slow_non_contiguous=True).then_inc(proj_here, 16)

            for u in range(UNITS):
                half, g = divmod(u, NG)
                sp.wait_ge(m_made, u + 1)
                for a in range(PARTS):
                    dst = q_stack[MROW + a:MROW + a + 1, half, GH * g:GH * (g + 1), :]
                    sp.dma_start(dst.rearrange("o h (b q) -> o (h b) q", q=P), m_parts[:, u % 2, a, :]).then_inc(m_rows, 16)

            sp.wait_ge(pv_done, STEPS)
            sp.dma_start(w13_rows[:, :, :], w13.rearrange("e (b p) c -> p (e b) c", p=P)).then_inc(experts_here, 16)
            sp.dma_start(w2_rows[:, :, :], w2.rearrange("e c i -> c e i")).then_inc(experts_here, 16)

            out_view = out[0].rearrange("(t p) c -> p t c", p=P)
            for th in range(2):
                sp.wait_ge(normed, th + 5)
                sp.dma_start(out_view[:, HB * th:HB * (th + 1), :], x_rows[:, HB * th:HB * (th + 1), :]).then_inc(stored, 16)
            sp.wait_ge(stored, 32)

        @block.gpsimd
        def _(pool):
            links = [0]

            def link(ins):
                links[0] += 1
                ins.then_inc(pool_chain, 1)
                pool.wait_ge(pool_chain, links[0])

            link(nc.gpsimd.memset(ident[:, :], 0.0))
            nc.gpsimd.affine_select(out=ident[:, :], in_=ident[:, :], compare_op=ALU.not_equal, fill=1.0, base=0,
                                    pattern=[[-1, P]], channel_multiplier=1).then_inc(ident_made, 1)
            pool.wait_ge(ident_made, 1)
            first, later = slice(0, GH), slice(GH, H)
            nc.gpsimd.memset(k_stack[64:P, first, :].bitcast(u32), ONES).then_inc(stack_set, 1)
            nc.gpsimd.memset(q_stack[64:P, 0, first, :].bitcast(u32), 0).then_inc(stack_set, 1)
            nc.gpsimd.memset(k_stack[64:P, later, :].bitcast(u32), ONES).then_inc(stack_set, 1)
            nc.gpsimd.memset(q_stack[64:P, 0, later, :].bitcast(u32), 0).then_inc(stack_set, 1)
            nc.gpsimd.memset(q_stack[64:P, 1, :, :].bitcast(u32), 0).then_inc(stack_set, 1)
            pool.wait_ge(stack_set, 5)

            for c in range(CTX_CHUNKS):
                _, col, width = context_chunk(c)
                pool.wait_ge(score_done, c + 1)
                nc.gpsimd.tensor_tensor(ctx_T_lo[:, col:col + width], stage[:, c % 2, 0:width],
                                        ctx_T_hi[:, col:col + width].bitcast(f32), ALU.subtract).then_inc(ctx_split, 1)

            pool.wait_ge(x_here, 16)
            pool.wait_ge(proj_here, 48)
            nc.gpsimd.tensor_tensor(pre_norm[:, :, :], x_rows[:, :, :],
                                    bias_p[:, :].unsqueeze(1).broadcast_to([P, TB, C]), ALU.add).then_inc(pre_bias, 1)
            for mask, n in ((lt4, 4), (lt8, NE)):
                link(nc.gpsimd.memset(mask[:, :, :], 1.0))
                nc.gpsimd.affine_select(out=mask[:, :, :], in_=mask[:, :, :], compare_op=ALU.is_ge, fill=0.0, base=-1,
                                        pattern=[[1, n], [-1, n]], channel_multiplier=0).then_inc(masks_made, 1)

            for e in range(NE):
                cols = slice(2 * INTER * e, 2 * INTER * (e + 1))
                pool.wait_ge(wt_taken, e + 1)
                nc.gpsimd.tensor_tensor(w13_T_lo[:, cols], stage[:, e % 2, :], w13_T_hi[:, cols].bitcast(f32),
                                        ALU.subtract).then_inc(wt_split, 1)

        @block.scalar
        def _(sc):
            sc.wait_ge(vec_ready, 1)
            nc.scalar.copy(x_T[:, HALF:N], pair_of_banks(0)[:, HALF:N]).then_inc(x_T_half, 1)

            sc.wait_ge(wqkv_here, 48)
            for n, (parts, made, w) in enumerate(((k_parts, k_made, 1), (q_parts, q_made, 0))):
                sc.wait_ge(vec_ready, n + 2)
                nc.scalar.activation(parts[:, 0, :], pair_of_banks(n + 1), ACT.Identity,
                                     bias=bias_col[:, w:w + 1]).then_inc(made, 1)
            for n, (parts, made, left) in enumerate(((k_parts, k_made, k_rest[:, :]), (q_parts, q_made, q_rest))):
                sc.wait_ge(vec_free, n + 2)
                nc.scalar.copy(parts[:, 1, :], left).then_inc(made, 1)

            for c in range(CTX_CHUNKS):
                _, col, width = context_chunk(c)
                sc.wait_ge(score_ready, c + 1)
                nc.scalar.copy(ctx_T_hi[:, col:col + width], score_bank(c)[:, 0:width])
                if c >= 2:
                    sc.wait_ge(ctx_split, c - 1)
                nc.scalar.copy(stage[:, c % 2, 0:width], score_bank(c)[:, 0:width]).then_inc(score_done, 1)

            def take_pv(u):
                sc.wait_ge(pv_done, KB * (u + 1))
                if u >= 2:
                    sc.wait_ge(o_read, u - 1)
                nc.scalar.copy(o_T[:, u % 2, :], pv_bank).then_inc(pv_taken, 1)

            for n in range(STEPS):
                for hh in range(GH):
                    i = CTX_CHUNKS + GH * n + hh
                    sc.wait_ge(score_ready, i + 1)
                    if n >= 2 and hh == 0:
                        sc.wait_ge(pv_done, n - 1)
                    nc.scalar.activation(probs[:, n % 2, hh, :], score_bank(i), ACT.Exp, scale=SCALE).then_inc(score_done, 1)
                if n and n % KB == 0:
                    take_pv(n // KB - 1)
            take_pv(UNITS - 1)

            def take_acc(th):
                sc.wait_ge(xa_summed, XJ * (th + 1))
                nc.scalar.copy(acc_T[:, th, :], acc_banks[th]).then_inc(acc_taken, 1)

            def router_exp(th):
                sc.wait_ge(shifted, th + 1)
                nc.scalar.activation(router[:, 1, :, :], router[:, 0, :, :], ACT.Exp).then_inc(exp_ready, 1)

            for k in range(XA):
                rows = FR if k % XJ == FB else P
                sc.wait_ge(xa_ready, k + 1)
                if k >= 3:
                    sc.wait_ge(xa_hid, k - 2)
                nc.scalar.activation(gelu[0:rows, k % 3, :], score_bank(k)[0:rows, :], ACT.Gelu_apprx_tanh).then_inc(xa_gelu, 1)
                w = weight_chunk_at(k)
                if w is not None:
                    sc.wait_ge(wt_ready, w + 1)
                    if w < NE:
                        nc.scalar.copy(w13_T_hi[:, 512 * w:512 * (w + 1)], weight_bank)
                        if w >= 2:
                            sc.wait_ge(wt_split, w - 1)
                        nc.scalar.copy(stage[:, w % 2, :], weight_bank).then_inc(wt_taken, 1)
                    else:
                        nc.scalar.copy(w2_T[:, 512 * (w - NE):512 * (w - NE + 1)], weight_bank).then_inc(wt_taken, 1)
                if k == ACC:
                    take_acc(0)
                if k == ACC + 12:
                    router_exp(0)
            take_acc(1)

            for u in range(4 * NE):
                sc.wait_ge(gate_ready, u + 1)
                if u >= 3:
                    sc.wait_ge(moe_act, u - 2)
                nc.scalar.activation(silu[:, u % 3, :], gate_up_banks[u % 2][:, 0, :], ACT.Silu).then_inc(moe_silu, 1)
                if u == 9:
                    router_exp(1)

        @block.tensor
        def _(pe):
            mm = nc.tensor.matmul
            jobs = [0]

            def vec_slot():
                n = jobs[0]
                jobs[0] += 1
                if n >= 2:
                    pe.wait_ge(vec_free, n - 1)
                return pair_of_banks(n)

            def half_transposes(slot, src, th):
                for b in range(HB):
                    last = nc.tensor.transpose(slot[:, P * b:P * (b + 1)], src[:, HB * th + b, :], ident[:, :])
                last.then_inc(vec_ready, 1)

            pe.wait_ge(ident_made, 1)
            pe.wait_ge(x_here, 16)
            slot = vec_slot()
            for tb in range(TB):
                last = nc.tensor.transpose(slot[:, P * tb:P * (tb + 1)], x_rows[:, tb, :], ident[:, :])
            last.then_inc(vec_ready, 1)

            pe.wait_ge(vec_free, 1)
            pe.wait_ge(x_T_half, 1)
            pe.wait_ge(wqkv_here, 48)
            for w in (1, 0):
                slot = vec_slot()
                for th in range(2):
                    hs = slice(HALF * th, HALF * (th + 1))
                    last = mm(slot[:, hs], wqkv[:, C * w:C * (w + 1)], x_T[:, hs], start=True, stop=True)
                last.then_inc(vec_ready, 1)
            slot = vec_slot()
            for tb in range(TB):
                last = mm(slot[:, P * tb:P * (tb + 1)], x_T[:, P * tb:P * (tb + 1)], wqkv[:, 2 * C:3 * C], start=True, stop=True)
            last.then_inc(vec_ready, 1)

            def context_transposes(c):
                blocks, _, _ = context_chunk(c)
                loads = {min(j, FB - 1) // (FB // CTX_LOADS) for j in blocks}
                for n in sorted(loads):
                    pe.wait_ge(ctx_here[n], 16)
                if blocks[-1] == FB:
                    pe.wait_ge(ctx_rest_here, 16)
                if c >= 3:
                    pe.wait_ge(score_done, c - 2)
                bank = score_bank(c)
                for n, j in enumerate(blocks):
                    if j < FB:
                        last = nc.tensor.transpose(bank[:, P * n:P * (n + 1)], ctx_rows[:, j, :], ident[:, :])
                    else:
                        last = nc.tensor.transpose(bank[:, P * n:P * n + FR], ctx_rest[:, :], ident[0:FR, 0:FR])
                last.then_inc(score_ready, 1)

            def max_tile(t):
                _, h, tb = max_tile_of(t)
                half, b = divmod(tb, HB)
                slot = vec_slot()
                for n in range(2):
                    last = mm(slot[:, HALF * n:HALF * (n + 1)], q_stack[:, half, h, P * b:P * (b + 1)],
                              k_stack[:, h, HALF * n:HALF * (n + 1)], start=True, stop=True)
                last.then_inc(vec_ready, 1)

            def max_rows(u):
                slot = vec_slot()
                pe.wait_ge(vec_free, jobs[0] - 1)
                nc.tensor.transpose(slot[0:UT, 0:P], neg_max[:, u, :], ident[:, :]).then_inc(vec_ready, 1)

            def attend_rows(u):
                slot = vec_slot()
                pe.wait_ge(pv_taken, u + 1)
                for b in range(HB):
                    last = nc.tensor.transpose(slot[:, P * b:P * (b + 1)], o_T[:, u % 2, P * b:P * (b + 1)], ident[:, :])
                last.then_inc(vec_ready, 1)

            def scores(n, hh):
                u, kb = divmod(n, KB)
                half, g = divmod(u, NG)
                i = CTX_CHUNKS + GH * n + hh
                h = GH * g + hh
                pe.wait_ge(score_done, i - 2)
                mm(score_bank(i), k_stack[:, h, P * kb:P * (kb + 1)], q_stack[:, half, h, :],
                   start=True, stop=True).then_inc(score_ready, 1)

            def weighted_sums(n):
                u, kb = divmod(n, KB)
                g = u % NG
                if kb == 0 and n:
                    pe.wait_ge(pv_taken, u)
                pe.wait_ge(score_done, CTX_CHUNKS + GH * (n + 1))
                for hh in range(GH):
                    last = mm(pv_bank[VW * hh:VW * (hh + 1), :], v_strip[:, kb, GH * g + hh, :], probs[:, n % 2, hh, :],
                              start=(kb == 0), stop=(kb == KB - 1))
                last.then_inc(pv_done, 1)

            def attended_T(th):
                slot = vec_slot()
                pe.wait_ge(vec_free, jobs[0] - 1)
                half_transposes(slot, att_rows, th)

            def project(th):
                slot = vec_slot()
                pe.wait_ge(vec_free, jobs[0] - 1)
                pe.wait_ge(proj_here, 48)
                for b in range(HB):
                    last = mm(slot[:, C * b:C * (b + 1)], att_T[:, P * b:P * (b + 1)], wproj[:, :], start=True, stop=True)
                last.then_inc(vec_ready, 1)

            def rows_to_T(th, norms):
                slot = vec_slot()
                pe.wait_ge(normed, norms)
                half_transposes(slot, x_rows, th)

            for c in range(3):
                context_transposes(c)
            c = 3
            pe.wait_ge(stacked[0], 16 * 2 * PARTS)
            for t in range(UT + LEAD):
                if t == UT:
                    max_rows(0)
                    pe.wait_ge(stacked[1], 16 * 2 * PARTS)
                max_tile(t)
                if t % 2 == 1 and c < CTX_CHUNKS:
                    context_transposes(c)
                    c += 1

            for n in range(STEPS):
                u, kb = divmod(n, KB)
                if kb == 0:
                    pe.wait_ge(m_rows, 16 * PARTS * (u + 1))
                if kb == 2 and u:
                    attend_rows(u - 1)
                if kb == KB - 2 and u + 1 < UNITS:
                    max_rows(u + 1)
                if n == 20:
                    pe.wait_ge(stacked[2], 16 * PARTS)
                if n == PROJ[0]:
                    attended_T(0)
                if n == PROJ[0] + 1:
                    project(0)
                if n == PROJ[0] + 4:
                    rows_to_T(0, 1)
                    x1_jobs = [jobs[0]]
                tiles = iter(max_tiles_at(n))
                for hh in range(GH):
                    scores(n, hh)
                    if hh == 2 and n:
                        weighted_sums(n - 1)
                    if hh < 2:
                        for t in tiles:
                            max_tile(t)
                            break
            weighted_sums(STEPS - 1)

            def cross(k):
                th, j = divmod(k, XJ)
                rows = FR if j == FB else P
                if j == 0:
                    pe.wait_ge(vec_free, x1_jobs[th])
                if k >= 3:
                    pe.wait_ge(xa_hid, k - 2)
                bank = score_bank(k)[0:rows, :]
                cs = slice(P * j, P * j + rows)
                mm(bank, ctx_T_hi[:, cs], x1_T_hi[th][:, :], start=True, stop=False)
                mm(bank, ctx_T_hi[:, cs], x1_T_lo[th][:, :], start=False, stop=False)
                mm(bank, ctx_T_lo[:, cs], x1_T_hi[th][:, :], start=False, stop=True).then_inc(xa_ready, 1)

            def cross_sum(k):
                th, j = divmod(k, XJ)
                rows = FR if j == FB else P
                pe.wait_ge(xa_hid, k + 1)
                lhs = ctx_rest[:, :] if j == FB else ctx_rows[:, j, :]
                mm(acc_banks[th], lhs, hid[0:rows, k % 3, :], start=(j == 0), stop=(j == FB)).then_inc(xa_summed, 1)

            def weight_transposes(w):
                if w == 0:
                    pe.wait_ge(experts_here, 32)
                else:
                    pe.wait_ge(wt_taken, w)
                for n in range(4):
                    if w < NE:
                        src = w13_rows[:, 4 * w + n, :]
                    else:
                        src = w2_rows[:, 2 * (w - NE) + n // 2, P * (n % 2):P * (n % 2 + 1)]
                    last = nc.tensor.transpose(weight_bank[:, P * n:P * (n + 1)], src, ident[:, :])
                last.then_inc(wt_ready, 1)

            def crossed_rows(th):
                slot = vec_slot()
                pe.wait_ge(acc_taken, th + 1)
                for b in range(HB):
                    last = nc.tensor.transpose(slot[:, P * b:P * (b + 1)], acc_T[:, th, P * b:P * (b + 1)], ident[:, :])
                last.then_inc(vec_ready, 1)

            def router_logits(th):
                slot = vec_slot()
                pe.wait_ge(x2_split, th + 1)
                for b in range(HB):
                    last = mm(slot[:, NE * b:NE * (b + 1)], x2_T[:, th, P * b:P * (b + 1)], gate_T[:, :], start=True, stop=True)
                last.then_inc(vec_ready, 1)

            pe.wait_ge(ctx_split, CTX_CHUNKS)
            pe.wait_ge(score_done, CTX_CHUNKS + GH * STEPS)
            for k in range(XA + LAG):
                if k < XA:
                    cross(k)
                if k == 1:
                    attend_rows(UNITS - 1)
                if k == LAG:
                    pe.wait_ge(pv_taken, UNITS)
                if k == PROJ[1]:
                    attended_T(1)
                if k == PROJ[1] + 2:
                    project(1)
                if k == PROJ[1] + 7:
                    rows_to_T(1, 2)
                    x1_jobs.append(jobs[0])
                w = weight_chunk_at(k)
                if w is not None:
                    weight_transposes(w)
                if k == ACC + 1:
                    crossed_rows(0)
                if k == ACC + 6:
                    rows_to_T(0, 3)
                if k == ACC + 9:
                    router_logits(0)
                if k >= LAG:
                    cross_sum(k - LAG)

            def gate_up(u):
                m, ib = divmod(u, 2)
                th, e = divmod(m, NE)
                for n, (ready, read) in enumerate(((gate_ready, moe_silu), (up_ready, moe_act))):
                    if u >= 2:
                        pe.wait_ge(read, u - 1)
                    col = 2 * INTER * e + INTER * n + P * ib
                    hi, lo = w13_T_hi[:, col:col + P], w13_T_lo[:, col:col + P]
                    bank = gate_up_banks[u % 2][:, n, :]
                    mm(bank, hi, x2_T_hi[:, th, :], start=True, stop=False)
                    mm(bank, hi, x2_T_lo[:, th, :], start=False, stop=False)
                    mm(bank, lo, x2_T_hi[:, th, :], start=False, stop=True).then_inc(ready, 1)

            def down(m):
                e = m % NE
                pe.wait_ge(moe_act, 2 * m + 2)
                if m == 1:
                    pe.wait_ge(acc_taken, 2)
                if m >= 2:
                    pe.wait_ge(down_taken, m - 1)
                for b in range(HB):
                    for ib in range(2):
                        last = mm(down_banks[m % 2][:, C * b:C * (b + 1)], act[:, 2 * (m % 2) + ib, P * b:P * (b + 1)],
                                  w2_T[:, (2 * e + ib) * C:(2 * e + ib + 1) * C], start=(ib == 0), stop=(ib == 1))
                last.then_inc(down_ready, 1)

            pe.wait_ge(wt_split, NE)
            pe.wait_ge(wt_taken, WT_CHUNKS)
            for m in range(2 * NE):
                if m == NE:
                    pe.wait_ge(x2_split, 2)
                gate_up(2 * m)
                gate_up(2 * m + 1)
                if m == 0:
                    crossed_rows(1)
                if m:
                    down(m - 1)
                if m == 2:
                    rows_to_T(1, 4)
                if m == 3:
                    router_logits(1)
            down(2 * NE - 1)

        @block.vector
        def _(ve):
            V = nc.vector
            links, jobs = [0], [0]

            def link(ins):
                links[0] += 1
                ins.then_inc(chain, 1)
                ve.wait_ge(chain, links[0])

            def vec_slot():
                n = jobs[0]
                jobs[0] += 1
                ve.wait_ge(vec_ready, n + 1)
                return pair_of_banks(n)

            link(V.memset(v_strip[:, :, :, :], 0.0))
            V.memset(v_strip[:, :, :, D:D + 1], 1.0).then_inc(strips_set, 1)

            slot = vec_slot()
            V.tensor_copy(x_T[:, 0:HALF], slot[:, 0:HALF]).then_inc(vec_free, 1)

            ve.wait_ge(wqkv_here, 48)
            for parts, made, left, w in ((k_parts, k_made, k_rest[:, :], 1), (q_parts, q_made, q_rest, 0)):
                slot = vec_slot()
                ve.wait_ge(made, 1)
                V.scalar_tensor_tensor(out=left, in0=slot, scalar=bias_col[:, w:w + 1], in1=parts[:, 0, :],
                                       op0=ALU.add, op1=ALU.subtract).then_inc(vec_free, 1)
            for parts, made, left in ((k_parts, k_made, k_rest[:, :]), (q_parts, q_made, q_rest)):
                ve.wait_ge(made, 2)
                V.tensor_tensor(parts[:, 2, :], left, parts[:, 1, :], ALU.subtract).then_inc(made, 1)

            slot = vec_slot()
            ve.wait_ge(strips_set, 1)
            for kb in range(KB):
                last = V.tensor_tensor(v_strip[:, kb, :, 0:D], slot[:, C * kb:C * (kb + 1)].rearrange("p (h d) -> p h d", d=D),
                                       bias_v[:, :].rearrange("p (h d) -> p h d", d=D), ALU.add)
            last.then_inc(vec_free, 1)

            def row_max(t):
                slot = vec_slot()
                u, i = divmod(t, UT)
                V.tensor_reduce(neg_max[:, u, i:i + 1], slot, axis=AX.X, op=ALU.max, negate=True).then_inc(vec_free, 1)

            def split_max(u):
                slot = vec_slot()
                src = slot[0:UT, 0:P]
                if u >= 2:
                    ve.wait_ge(m_rows, 16 * PARTS * (u - 1))
                link(V.tensor_copy(m_parts[:, u % 2, 0, :], src))
                V.tensor_tensor(m_rest[:, u % 2, :], src, m_parts[:, u % 2, 0, :], ALU.subtract).then_inc(vec_free, 1)
                ve.wait_ge(vec_free, jobs[0])
                link(V.tensor_copy(m_parts[:, u % 2, 1, :], m_rest[:, u % 2, :]))
                V.tensor_tensor(m_parts[:, u % 2, 2, :], m_rest[:, u % 2, :], m_parts[:, u % 2, 1, :],
                                ALU.subtract).then_inc(m_made, 1)

            def divide(u):
                half, g = divmod(u, NG)
                slot = vec_slot()
                sums = slot[:, 0:HALF].rearrange("p (s w) -> p s w", w=VW)
                V.reciprocal(recip[:, u % 2, :].unsqueeze(2), sums[:, :, D:D + 1]).then_inc(o_read, 1)
                ve.wait_ge(o_read, u + 1)
                dst = att_rows[:, HB * half:HB * (half + 1), GH * D * g:GH * D * (g + 1)]
                over = recip[:, u % 2, :].rearrange("p (b h) -> p b h", h=GH).unsqueeze(3).broadcast_to([P, HB, GH, D])
                V.tensor_tensor(dst.rearrange("p b (h d) -> p b h d", d=D), sums[:, :, 0:D].rearrange("p (b h) d -> p b h d", h=GH),
                                over, ALU.mult).then_inc(vec_free, 1)

            def flat(rows, th):
                return rows[:, HB * th:HB * (th + 1), :].rearrange("p t c -> p (t c)")

            def norm_stats(th):
                for b in range(HB):
                    last = V.bn_stats(stats[:, b, :], pre_norm[:, HB * th + b, :])
                link(last)
                for b in range(HB):
                    last = V.bn_aggr(mean_var[:, b, :], stats[:, b, :])
                link(last)

            def norm_root():
                var, r, t, t2 = (norm_s[:, i, :] for i in range(4))
                link(V.tensor_scalar(var, mean_var[:, :, 1], EPS, None, ALU.add))
                link(V.tensor_scalar(r.bitcast(i32), var.bitcast(i32), -0.5, float(0x5F3759DF), ALU.mult, ALU.add))
                for _ in range(4):
                    link(V.scalar_tensor_tensor(out=t, in0=r, scalar=-0.5, in1=r, op0=ALU.mult, op1=ALU.mult))
                    link(V.tensor_tensor(t2, t, var, ALU.mult))
                    link(V.scalar_tensor_tensor(out=r, in0=t2, scalar=1.5, in1=r, op0=ALU.add, op1=ALU.mult))

            def norm_apply(th):
                for b in range(HB):
                    tb = HB * th + b
                    last = V.tensor_scalar(x_rows[:, tb, :], pre_norm[:, tb, :], mean_var[:, b, 0:1], norm_s[:, 1, b:b + 1],
                                           ALU.subtract, ALU.mult)
                last.then_inc(normed, 1)

            def take_attended():
                slot = vec_slot()
                V.tensor_copy(att_T[:, :], slot[:, 0:HALF]).then_inc(vec_free, 1)

            def add_projected(th):
                slot = vec_slot()
                ve.wait_ge(pre_bias, 1)
                V.tensor_tensor(flat(pre_norm, th), slot[:, 0:HALF], flat(pre_norm, th), ALU.add).then_inc(vec_free, 1)
                ve.wait_ge(vec_free, jobs[0])

            def split_x1(th):
                slot = vec_slot()
                link(V.tensor_copy(x1_T_hi[th][:, :], slot[:, 0:HALF]))
                V.tensor_tensor(x1_T_lo[th][:, :], slot[:, 0:HALF], x1_T_hi[th][:, :].bitcast(f32), ALU.subtract).then_inc(vec_free, 1)

            for t in range(UT):
                row_max(t)
            split_max(0)
            for t in range(UT, UT + LEAD):
                row_max(t)
            for n in range(STEPS):
                u, kb = divmod(n, KB)
                if kb == 2 and u:
                    divide(u - 1)
                if kb == KB - 2 and u + 1 < UNITS:
                    split_max(u + 1)
                if n == PROJ[0]:
                    take_attended()
                if n == PROJ[0] + 1:
                    add_projected(0)
                    norm_stats(0)
                if n == PROJ[0] + 2:
                    norm_root()
                if n == PROJ[0] + 3:
                    norm_apply(0)
                if n == PROJ[0] + 4:
                    split_x1(0)
                for t in max_tiles_at(n):
                    row_max(t)

            def add_crossed(th):
                slot = vec_slot()
                V.tensor_tensor(flat(pre_norm, th), slot[:, 0:HALF], flat(x_rows, th), ALU.add).then_inc(vec_free, 1)
                ve.wait_ge(vec_free, jobs[0])

            def split_x2(th):
                slot = vec_slot()
                V.tensor_copy(x2_T[:, th, :], slot[:, 0:HALF]).then_inc(vec_free, 1)
                ve.wait_ge(vec_free, jobs[0])
                link(V.tensor_copy(x2_T_hi[:, th, :], x2_T[:, th, :]))
                V.tensor_tensor(x2_T_lo[:, th, :], x2_T[:, th, :], x2_T_hi[:, th, :].bitcast(f32), ALU.subtract).then_inc(x2_split, 1)

            def over_e(a):
                return a.unsqueeze(2).broadcast_to([P, HB, NE])

            sh, ex, sc, masked, sel, wt = (router[:, i, :, :] for i in range(6))
            groups, rank4, rank8 = router[:, 6, :, 0:4], router[:, 6, :, 4:8], router[:, 7, :, :]

            def route_shift():
                slot = vec_slot()
                V.tensor_copy(logits[:, :, :], slot[:, 0:HB * NE].rearrange("p (t e) -> p t e", e=NE)).then_inc(vec_free, 1)
                ve.wait_ge(vec_free, jobs[0])
                link(V.tensor_reduce(small[:, 0, :], logits[:, :, :], axis=AX.X, op=ALU.max))
                V.tensor_tensor(sh, logits[:, :, :], over_e(small[:, 0, :]), ALU.subtract).then_inc(shifted, 1)

            def rank(dst, val, lt, n):
                gt = pair[:, 0, 0:HB * n * n].rearrange("p (t j i) -> p t j i", j=n, i=n)
                ge = pair[:, 1, 0:HB * n * n].rearrange("p (t j i) -> p t j i", j=n, i=n)
                vi = val.unsqueeze(2).broadcast_to([P, HB, n, n])
                vj = val.unsqueeze(3).broadcast_to([P, HB, n, n])
                V.tensor_tensor(gt, vi, vj, ALU.is_gt)
                link(V.tensor_tensor(ge, vi, vj, ALU.is_ge))
                link(V.tensor_tensor(ge, ge, lt.unsqueeze(1).broadcast_to([P, HB, n, n]), ALU.mult))
                link(V.tensor_tensor(gt, gt, ge, ALU.max))
                link(V.tensor_reduce(dst, gt, axis=AX.X, op=ALU.add))

            def route_groups(th):
                ve.wait_ge(exp_ready, th + 1)
                link(V.tensor_reduce(small[:, 1, :], ex, axis=AX.X, op=ALU.add))
                link(V.reciprocal(small[:, 2, :], small[:, 1, :]))
                link(V.tensor_tensor(sc, ex, over_e(small[:, 2, :]), ALU.mult))
                link(V.tensor_tensor(groups, sc[:, :, 0::2], sc[:, :, 1::2], ALU.max))
                ve.wait_ge(masks_made, 2)
                rank(rank4, groups, lt4[:, :, :], 4)
                link(V.tensor_scalar(groups, rank4, 2.0, None, ALU.is_lt))
                link(V.tensor_tensor(masked.rearrange("p t (g o) -> p t g o", o=2), sc.rearrange("p t (g o) -> p t g o", o=2),
                                     groups.unsqueeze(3).broadcast_to([P, HB, 4, 2]), ALU.mult))

            def route_experts(th):
                rank(rank8, masked, lt8[:, :, :], NE)
                link(V.tensor_scalar(sel, rank8, 2.0, None, ALU.is_lt))
                link(V.tensor_tensor(wt, masked, sel, ALU.mult))
                link(V.tensor_reduce(small[:, 3, :], wt, axis=AX.X, op=ALU.add))
                link(V.reciprocal(small[:, 0, :], small[:, 3, :]))
                link(V.tensor_tensor(combine[:, HB * th:HB * (th + 1), :], wt, over_e(small[:, 0, :]), ALU.mult))

            for k in range(XA):
                rows = FR if k % XJ == FB else P
                ve.wait_ge(xa_gelu, k + 1)
                if k >= 3:
                    ve.wait_ge(xa_summed, k - 2)
                V.tensor_tensor(hid[0:rows, k % 3, :], gelu[0:rows, k % 3, :], score_bank(k)[0:rows, :], ALU.mult).then_inc(xa_hid, 1)
                if k == 1:
                    divide(UNITS - 1)
                if k == PROJ[1]:
                    take_attended()
                if k == PROJ[1] + 2:
                    add_projected(1)
                if k == PROJ[1] + 3:
                    norm_stats(1)
                if k == PROJ[1] + 4:
                    norm_root()
                if k == PROJ[1] + 6:
                    norm_apply(1)
                if k == PROJ[1] + 7:
                    split_x1(1)
                if k == ACC + 1:
                    add_crossed(0)
                if k == ACC + 2:
                    norm_stats(0)
                if k == ACC + 3:
                    norm_root()
                if k == ACC + 5:
                    norm_apply(0)
                if k == ACC + 6:
                    split_x2(0)
                if k == ACC + 9:
                    route_shift()
                if k == ACC + 14:
                    route_groups(0)
                if k == ACC + 17:
                    route_experts(0)

            def hidden(u):
                m, ib = divmod(u, 2)
                ve.wait_ge(moe_silu, u + 1)
                ve.wait_ge(up_ready, u + 1)
                if m >= 2:
                    ve.wait_ge(down_ready, m - 1)
                V.tensor_tensor(act[:, 2 * (m % 2) + ib, :], silu[:, u % 3, :], gate_up_banks[u % 2][:, 1, :],
                                ALU.mult).then_inc(moe_act, 1)

            def add_expert(m):
                th, e = divmod(m, NE)
                ve.wait_ge(down_ready, m + 1)
                if e:
                    ve.wait_ge(down_taken, m)
                for b in range(HB):
                    tb = HB * th + b
                    base = pre_norm if e else x_rows
                    last = V.scalar_tensor_tensor(out=pre_norm[:, tb, :], in0=down_banks[m % 2][:, C * b:C * (b + 1)],
                                                  scalar=combine[:, tb, e:e + 1], in1=base[:, tb, :], op0=ALU.mult, op1=ALU.add)
                last.then_inc(down_taken, 1)

            for m in range(2 * NE):
                hidden(2 * m)
                hidden(2 * m + 1)
                if m == 0:
                    add_crossed(1)
                    norm_stats(1)
                if m:
                    add_expert(m - 1)
                if m == 1:
                    norm_root()
                    norm_apply(1)
                if m == 2:
                    split_x2(1)
                if m == 3:
                    route_shift()
                if m == 5:
                    route_groups(1)
                if m == 6:
                    route_experts(1)
                if m == NE + 1:
                    ve.wait_ge(down_taken, NE)
                    norm_stats(0)
                if m == NE + 2:
                    norm_root()
                if m == NE + 3:
                    norm_apply(0)
            add_expert(2 * NE - 1)
            ve.wait_ge(down_taken, 2 * NE)
            norm_stats(1)
            norm_root()
            norm_apply(1)


_INS = ['x', 'ctx_1024', 'L0_attn_qkv_w', 'L0_attn_qkv_b', 'L0_attn_proj_w', 'L0_attn_proj_b', 'L0_ffn_gate_w',
        'L0_ffn_w13_weight', 'L0_ffn_w2_weight']


def kernel(**inputs):
    import numpy as _np
    import concourse.bacc as _bacc
    from concourse import mybir as _mybir
    from concourse.bass_utils import run_bass_kernel_spmd as _run

    nc = _bacc.Bacc("TRN2", target_bir_lowering=False, num_devices=1)
    arrays, args = {}, []
    for name in _INS:
        a = _np.ascontiguousarray(inputs[name])
        arrays[f"in_{name}"] = a
        args.append(nc.dram_tensor(f"in_{name}", a.shape, _mybir.dt.from_np(a.dtype), kind="ExternalInput").ap())
    args.append(nc.dram_tensor("out_0", (1, N, C), _mybir.dt.float32, kind="ExternalOutput").ap())
    args.append(nc.dram_tensor("kept_k", (PARTS, D, H, N), _mybir.dt.bfloat16, kind="Internal").ap())
    args.append(nc.dram_tensor("kept_q", (2, PARTS, D, H, HALF), _mybir.dt.bfloat16, kind="Internal").ap())
    build(nc, *args)
    r = _run(nc, [arrays], core_ids=[0])
    return r.results[0]["out_0"]
```

```python
import concourse.bass as bass
from concourse import mybir
from contextlib import ExitStack


P = 128
N = 1024
C = 128
H = 16
D = C // H
F = 6404
NE = 8
INTER = 256
TB = N // P
HALF = N // 2
HB = TB // 2
EPS = 1e-5
SCALE = float(D) ** -0.5

PARTS = 3
PAIRS = PARTS * D
MROW = PARTS * PAIRS
ONES = 0x3F803F80
GH = 4
NG = H // GH
VW = 32
KB = N // P
UNITS = 2 * NG
STEPS = UNITS * KB
UT = GH * HB
LEAD = 4
MAX_TILES = UNITS * UT

FB = F // P
FR = F - FB * P
CTX_CHUNKS = -(-(FB + 1) // 4)
CTX_EARLY = 5
CTX_LOADS = 5
XJ = FB + 1
XA = 2 * XJ
LAG = 4
WT_CHUNKS = NE + NE // 2

PROJ = (54, 3)
ACC = XJ + LAG
WT_FIRST, WT_EVERY = 10, 6


def max_tiles_at(n):
    first = UT + LEAD + 2 * n
    return range(min(first, MAX_TILES), min(first + 2, MAX_TILES))


def max_tile_of(t):
    u, i = divmod(t, UT)
    half, g = divmod(u, NG)
    return u, GH * g + i // HB, HB * half + i % HB


def context_chunk(c):
    blocks = range(4 * c, min(4 * c + 4, FB + 1))
    return blocks, 4 * c * P, min(4 * P, F - 4 * c * P)


def last_of_chunk(k):
    j = k % XJ
    return j % 4 == 3 or j == FB


def chunk_of(k):
    th, j = divmod(k, XJ)
    return CTX_CHUNKS * th + j // 4


def first_tile_of(c):
    return XJ * (c // CTX_CHUNKS) + 4 * (c % CTX_CHUNKS)


def weight_chunk_at(k):
    w = (k - WT_FIRST) // WT_EVERY
    return w if k >= WT_FIRST and (k - WT_FIRST) % WT_EVERY == 0 and w < WT_CHUNKS else None


def build(nc, x, ctx, qkv_w, qkv_b, proj_w, proj_b, gate_w, w13, w2, out, kept_k, kept_q):
    f32 = mybir.dt.float32
    f32r = mybir.dt.float32r
    bf16 = mybir.dt.bfloat16
    u32 = mybir.dt.uint32
    i32 = mybir.dt.int32
    ALU = mybir.AluOpType
    ACT = mybir.ActivationFunctionType
    AX = mybir.AxisListType

    stack = ExitStack()
    with stack:
        def sb(name, shape, dt, scope=stack):
            return scope.enter_context(nc.sbuf_tensor(name, shape, dt))

        def sem(name):
            return stack.enter_context(nc.semaphore(name))

        ident = sb("ident", [P, P], f32)
        x_rows = sb("x_rows", [P, TB, C], f32)
        pre_norm = sb("pre_norm", [P, TB, C], f32)
        gate_T = sb("gate_T", [P, NE], f32)
        lt4 = sb("lt4", [P, 4, 4], f32)
        lt8 = sb("lt8", [P, NE, NE], f32)
        stats = sb("stats", [P, HB, 6], f32)
        mean_var = sb("mean_var", [P, HB, 2], f32)
        norm_s = sb("norm_s", [P, 4, HB], f32)
        ctx_rows = sb("ctx_rows", [P, FB, C], f32)
        ctx_rest = sb("ctx_rest", [FR, C], f32)
        ctx_T_hi = sb("ctx_T_hi", [P, F], f32r)
        ctx_T_lo = sb("ctx_T_lo", [P, F], f32r)
        stage = sb("stage", [P, 2, 512], f32)
        recip = sb("recip", [P, 2, HB * GH], f32)
        x1a_T_hi = sb("x1a_T_hi", [P, HALF], f32r)
        x1a_T_lo = sb("x1a_T_lo", [P, HALF], f32r)

        att = ExitStack()
        q_stack = sb("q_stack", [P, 2, H, HALF], bf16, att)
        k_stack = sb("k_stack", [P, H, N], bf16, att)
        v_strip = sb("v_strip", [P, KB, H, VW], f32, att)
        att_rows = sb("att_rows", [P, TB, C], f32, att)
        att_T = sb("att_T", [P, HALF], f32, att)
        wqkv = sb("wqkv", [P, 3 * C], f32, att)
        bias_col = sb("bias_col", [P, 2], f32, att)
        bias_v = sb("bias_v", [P, C], f32, att)
        wproj = sb("wproj", [P, C], f32, att)
        bias_p = sb("bias_p", [P, C], f32, att)
        neg_max = sb("neg_max", [P, UNITS, UT], f32, att)
        m_parts = sb("m_parts", [UT, 2, PARTS, P], bf16, att)
        m_rest = sb("m_rest", [UT, 2, P], f32, att)
        pre = ExitStack()
        x_T = sb("x_T", [P, N], f32, pre)
        q_parts = sb("q_parts", [P, PARTS, N], bf16, pre)
        k_parts = sb("k_parts", [P, PARTS, N], bf16, pre)
        k_rest = sb("k_rest", [P, N], f32, pre)
        q_rest = att_rows[:, :, :].rearrange("p t c -> p (t c)")
        pre.close()
        probs = sb("probs", [P, 2, GH, HALF], f32, att)
        o_T = sb("o_T", [P, 2, HALF], f32, att)
        att.close()

        cross_only = ExitStack()
        gelu = sb("gelu", [P, 2, HALF], f32, cross_only)
        hid = sb("hid", [P, 3, HALF], f32, cross_only)
        hid_hi = sb("hid_hi", [P, 4, HALF], f32r, cross_only)
        hid_lo = sb("hid_lo", [P, 4, HALF], f32r, cross_only)
        ctx_hi = sb("ctx_hi", [P, 2, 4 * C], f32r, cross_only)
        ctx_lo = sb("ctx_lo", [P, 2, 4 * C], f32r, cross_only)
        cross_only.close()
        experts_only = ExitStack()
        silu = sb("silu", [P, 3, HALF], f32, experts_only)
        act = sb("act", [P, 4, HALF], f32, experts_only)
        room = sb("room", [P, 10, HALF], f32, experts_only)
        w13_T_hi = sb("w13_T_hi", [P, NE * 2 * INTER], f32r, experts_only)
        w13_T_lo = sb("w13_T_lo", [P, NE * 2 * INTER], f32r, experts_only)
        w2_T = sb("w2_T", [P, NE * 2 * C], f32, experts_only)
        x1b_T_hi = sb("x1b_T_hi", [P, HALF], f32r, experts_only)
        x1b_T_lo = sb("x1b_T_lo", [P, HALF], f32r, experts_only)
        acc_T = sb("acc_T", [P, 2, HALF], f32, experts_only)
        router = sb("router", [P, 8, HB, NE], f32, experts_only)
        pair = sb("pair", [P, 2, HB * NE * NE], f32, experts_only)
        small = sb("small", [P, 4, HB], f32, experts_only)
        logits = sb("logits", [P, HB, NE], f32, experts_only)
        combine = sb("combine", [P, TB, NE], f32, experts_only)
        x2_T = sb("x2_T", [P, 2, HALF], f32, experts_only)
        rows_only = ExitStack()
        w13_rows = sb("w13_rows", [P, 4 * NE, C], f32, rows_only)
        w2_rows = sb("w2_rows", [P, NE, INTER], f32, rows_only)
        rows_only.close()
        x2_T_hi = sb("x2_T_hi", [P, 2, HALF], f32r, experts_only)
        x2_T_lo = sb("x2_T_lo", [P, 2, HALF], f32r, experts_only)
        experts_only.close()
        x1_T_hi = (x1a_T_hi, x1b_T_hi)
        x1_T_lo = (x1a_T_lo, x1b_T_lo)

        psum = stack.enter_context(nc.psum_tensor("psum", [P, 8, 512], f32))

        def pair_of_banks(n):
            b = 2 * (n % 2)
            return psum[:, b:b + 2, :].rearrange("p b c -> p (b c)")

        def score_bank(n):
            return psum[:, 4 + n % 3, :]

        pv_bank = psum[:, 7, :]
        acc_banks = (psum[:, 7, :], psum[:, 3, :])
        weight_bank = psum[:, 1, :]
        gate_up_banks = (psum[:, 4:6, :], psum[:, 6:8, :])
        down_banks = (psum[:, 1, :], psum[:, 3, :])

        x_here = sem("x_here")
        wqkv_here = sem("wqkv_here")
        proj_here = sem("proj_here")
        ctx_here = [sem(f"ctx_here{n}") for n in range(CTX_LOADS)]
        ctx_rest_here = sem("ctx_rest_here")
        experts_here = sem("experts_here")
        ident_made = sem("ident_made")
        strips_set = sem("strips_set")
        masks_made = sem("masks_made")
        pre_bias = sem("pre_bias")
        stack_set = sem("stack_set")
        x_T_half = sem("x_T_half")
        k_made = sem("k_made")
        q_made = sem("q_made")
        k_kept = sem("k_kept")
        q_kept = [sem(f"q_kept{half}") for half in range(2)]
        stacked = [sem(f"stacked{n}") for n in range(3)]
        vec_ready = sem("vec_ready")
        vec_free = sem("vec_free")
        chain = sem("chain")
        pool_chain = sem("pool_chain")
        m_made = sem("m_made")
        m_rows = sem("m_rows")
        score_ready = sem("score_ready")
        score_done = sem("score_done")
        ctx_split = sem("ctx_split")
        pv_done = sem("pv_done")
        pv_taken = sem("pv_taken")
        o_read = sem("o_read")
        xa_ready = sem("xa_ready")
        xa_gelu = sem("xa_gelu")
        xa_hid = sem("xa_hid")
        xa_high = sem("xa_high")
        xa_low = (sem("xa_low_even"), sem("xa_low_odd"))
        xa_summed = sem("xa_summed")
        ctx_high = sem("ctx_high")
        ctx_low = sem("ctx_low")
        wt_ready = sem("wt_ready")
        wt_taken = sem("wt_taken")
        wt_split = sem("wt_split")
        acc_taken = sem("acc_taken")
        x2_split = sem("x2_split")
        shifted = sem("shifted")
        exp_ready = sem("exp_ready")
        gate_ready = sem("gate_ready")
        up_ready = sem("up_ready")
        moe_silu = sem("moe_silu")
        moe_act = sem("moe_act")
        down_ready = sem("down_ready")
        down_taken = sem("down_taken")
        normed = sem("normed")
        stored = sem("stored")

        block = stack.enter_context(nc.Block())

        @block.sync
        def _(sp):
            def stack_k(heads, n):
                sp.wait_ge(stack_set, 2 * n + 1)
                sp.wait_ge(k_kept, 16 * PARTS)
                src = kept_k.rearrange("j d h t -> (j d) h t")[:, heads, :].rearrange("r h t -> r (h t)")
                src = src.unsqueeze(0).broadcast_to([PARTS] + list(src.shape))
                sp.dma_start(k_stack[0:MROW, heads, :].rearrange("r h t -> r (h t)"), src).then_inc(stacked[n], 16)

            def stack_q(half, heads, n):
                sp.wait_ge(stack_set, 2 * n + 2 if n < 2 else 5)
                sp.wait_ge(q_kept[half], 16 * PARTS)
                for a in range(PARTS):
                    src = kept_q[half, a][:, heads, :].rearrange("d h t -> d (h t)")
                    src = src.unsqueeze(0).broadcast_to([PARTS] + list(src.shape))
                    sp.dma_start(q_stack[PAIRS * a:PAIRS * (a + 1), half, heads, :].rearrange("r h t -> r (h t)"),
                                 src).then_inc(stacked[n], 16)

            x_view = x[0].rearrange("(t p) c -> p t c", p=P)
            sp.dma_start(x_rows[:, :, :], x_view).then_inc(x_here, 16)
            sp.dma_start(wqkv[:, :], qkv_w).then_inc(wqkv_here, 16)
            sp.dma_start(bias_col[:, :], qkv_b[0:2 * C].rearrange("(j p) -> p j", p=P),
                         allow_slow_non_contiguous=True).then_inc(wqkv_here, 16)
            sp.dma_start(bias_v[:, :], qkv_b[2 * C:3 * C].partition_broadcast(P)).then_inc(wqkv_here, 16)
            ctx_view = ctx[0, 0:FB * P, :].rearrange("(p j) c -> p j c", j=FB)
            per = FB // CTX_LOADS
            for n in range(CTX_LOADS):
                if n == 2:
                    for part in range(PARTS):
                        sp.wait_ge(k_made, part + 1)
                        sp.dma_start(kept_k[part].rearrange("d h t -> h d t"), k_parts[:, part, :]).then_inc(k_kept, 16)
                        sp.wait_ge(q_made, part + 1)
                        sp.dma_start(kept_q[0, part].rearrange("d h t -> h d t"),
                                     q_parts[:, part, 0:HALF]).then_inc(q_kept[0], 16)
                    stack_k(slice(0, GH), 0)
                    stack_q(0, slice(0, GH), 0)
                sp.dma_start(ctx_rows[:, n * per:(n + 1) * per, :],
                             ctx_view[:, n * per:(n + 1) * per, :]).then_inc(ctx_here[n], 16)
            for part in range(PARTS):
                sp.dma_start(kept_q[1, part].rearrange("d h t -> h d t"),
                             q_parts[:, part, HALF:N]).then_inc(q_kept[1], 16)
            sp.wait_ge(q_kept[1], 16 * PARTS)
            stack_k(slice(GH, H), 1)
            stack_q(0, slice(GH, H), 1)
            stack_q(1, slice(0, H), 2)
            sp.dma_start(ctx_rest[:, :], ctx[0, FB * P:F, :]).then_inc(ctx_rest_here, 16)
            sp.dma_start(wproj[:, :], proj_w).then_inc(proj_here, 16)
            sp.dma_start(bias_p[:, :], proj_b.partition_broadcast(P)).then_inc(proj_here, 16)
            sp.dma_start(gate_T[:, :], gate_w.rearrange("e c -> c e"), allow_slow_non_contiguous=True).then_inc(proj_here, 16)

            for u in range(UNITS):
                half, g = divmod(u, NG)
                sp.wait_ge(m_made, u + 1)
                for a in range(PARTS):
                    dst = q_stack[MROW + a:MROW + a + 1, half, GH * g:GH * (g + 1), :]
                    sp.dma_start(dst.rearrange("o h (b q) -> o (h b) q", q=P), m_parts[:, u % 2, a, :]).then_inc(m_rows, 16)

            sp.wait_ge(pv_done, STEPS)
            sp.dma_start(w13_rows[:, :, :], w13.rearrange("e (b p) c -> p (e b) c", p=P)).then_inc(experts_here, 16)
            sp.wait_ge(o_read, UNITS)
            sp.dma_start(w2_rows[:, :, :], w2.rearrange("e c i -> c e i")).then_inc(experts_here, 16)

            out_view = out[0].rearrange("(t p) c -> p t c", p=P)
            for th in range(2):
                sp.wait_ge(normed, th + 5)
                sp.dma_start(out_view[:, HB * th:HB * (th + 1), :], x_rows[:, HB * th:HB * (th + 1), :]).then_inc(stored, 16)
            sp.wait_ge(stored, 32)

        @block.gpsimd
        def _(pool):
            links = [0]

            def link(ins):
                links[0] += 1
                ins.then_inc(pool_chain, 1)
                pool.wait_ge(pool_chain, links[0])

            link(nc.gpsimd.memset(ident[:, :], 0.0))
            nc.gpsimd.affine_select(out=ident[:, :], in_=ident[:, :], compare_op=ALU.not_equal, fill=1.0, base=0,
                                    pattern=[[-1, P]], channel_multiplier=1).then_inc(ident_made, 1)
            pool.wait_ge(ident_made, 1)
            first, later = slice(0, GH), slice(GH, H)
            nc.gpsimd.memset(k_stack[64:P, first, :].bitcast(u32), ONES).then_inc(stack_set, 1)
            nc.gpsimd.memset(q_stack[64:P, 0, first, :].bitcast(u32), 0).then_inc(stack_set, 1)
            nc.gpsimd.memset(k_stack[64:P, later, :].bitcast(u32), ONES).then_inc(stack_set, 1)
            nc.gpsimd.memset(q_stack[64:P, 0, later, :].bitcast(u32), 0).then_inc(stack_set, 1)
            nc.gpsimd.memset(q_stack[64:P, 1, :, :].bitcast(u32), 0).then_inc(stack_set, 1)
            pool.wait_ge(stack_set, 5)

            for c in range(CTX_CHUNKS):
                _, col, width = context_chunk(c)
                pool.wait_ge(score_done, c + 1)
                nc.gpsimd.tensor_tensor(ctx_T_lo[:, col:col + width], stage[:, c % 2, 0:width],
                                        ctx_T_hi[:, col:col + width].bitcast(f32), ALU.subtract).then_inc(ctx_split, 1)

            pool.wait_ge(x_here, 16)
            pool.wait_ge(proj_here, 48)
            nc.gpsimd.tensor_tensor(pre_norm[:, :, :], x_rows[:, :, :],
                                    bias_p[:, :].unsqueeze(1).broadcast_to([P, TB, C]), ALU.add).then_inc(pre_bias, 1)
            for mask, n in ((lt4, 4), (lt8, NE)):
                link(nc.gpsimd.memset(mask[:, :, :], 1.0))
                nc.gpsimd.affine_select(out=mask[:, :, :], in_=mask[:, :, :], compare_op=ALU.is_ge, fill=0.0, base=-1,
                                        pattern=[[1, n], [-1, n]], channel_multiplier=0).then_inc(masks_made, 1)

            def low_rows(c):
                blocks, _, _ = context_chunk(c % CTX_CHUNKS)
                whole = [b for b in blocks if b < FB]
                cols = slice(0, C * len(whole))
                rows = ctx_rows[:, whole[0]:whole[-1] + 1, :].rearrange("p j c -> p (j c)")
                pool.wait_ge(ctx_high, c + 1)
                low = nc.gpsimd.tensor_tensor(ctx_lo[:, c % 2, cols], rows, ctx_hi[:, c % 2, cols].bitcast(f32), ALU.subtract)
                if blocks[-1] == FB:
                    link(low)
                    at = slice(C * len(whole), C * len(whole) + C)
                    low = nc.gpsimd.tensor_tensor(ctx_lo[0:FR, c % 2, at], ctx_rest[:, :],
                                                  ctx_hi[0:FR, c % 2, at].bitcast(f32), ALU.subtract)
                low.then_inc(ctx_low, 1)
                pool.wait_ge(ctx_low, c + 1)

            def low_weights(e):
                cols = slice(2 * INTER * e, 2 * INTER * (e + 1))
                pool.wait_ge(wt_taken, e + 1)
                nc.gpsimd.tensor_tensor(w13_T_lo[:, cols], stage[:, e % 2, :], w13_T_hi[:, cols].bitcast(f32),
                                        ALU.subtract).then_inc(wt_split, 1)
                pool.wait_ge(wt_split, e + 1)

            pool.wait_ge(pv_done, STEPS)
            low_rows(0)
            for k in range(XA):
                if last_of_chunk(k) and k + 1 < XA:
                    low_rows(chunk_of(k) + 1)
                if k % 2 == 1:
                    rows = FR if k % XJ == FB else P
                    pool.wait_ge(xa_high, k + 1)
                    nc.gpsimd.tensor_tensor(hid_lo[0:rows, k % 4, :], hid[0:rows, k % 3, :],
                                            hid_hi[0:rows, k % 4, :].bitcast(f32), ALU.subtract).then_inc(xa_low[1], 1)
                    pool.wait_ge(xa_low[1], k // 2 + 1)
                w = weight_chunk_at(k)
                if w is not None and w < NE:
                    low_weights(w)

        @block.scalar
        def _(sc):
            sc.wait_ge(vec_ready, 1)
            nc.scalar.copy(x_T[:, HALF:N], pair_of_banks(0)[:, HALF:N]).then_inc(x_T_half, 1)

            sc.wait_ge(wqkv_here, 48)
            for n, (parts, made, w) in enumerate(((k_parts, k_made, 1), (q_parts, q_made, 0))):
                sc.wait_ge(vec_ready, n + 2)
                nc.scalar.activation(parts[:, 0, :], pair_of_banks(n + 1), ACT.Identity,
                                     bias=bias_col[:, w:w + 1]).then_inc(made, 1)
            for n, (parts, made, left) in enumerate(((k_parts, k_made, k_rest[:, :]), (q_parts, q_made, q_rest))):
                sc.wait_ge(vec_free, n + 2)
                nc.scalar.copy(parts[:, 1, :], left).then_inc(made, 1)

            def take_context(c):
                _, col, width = context_chunk(c)
                sc.wait_ge(score_ready, c + 1)
                nc.scalar.copy(ctx_T_hi[:, col:col + width], score_bank(c)[:, 0:width])
                if c >= 2:
                    sc.wait_ge(ctx_split, c - 1)
                nc.scalar.copy(stage[:, c % 2, 0:width], score_bank(c)[:, 0:width]).then_inc(score_done, 1)

            for c in range(CTX_CHUNKS):
                take_context(c)

            def take_pv(u):
                sc.wait_ge(pv_done, KB * (u + 1))
                if u >= 2:
                    sc.wait_ge(o_read, u - 1)
                nc.scalar.copy(o_T[:, u % 2, :], pv_bank).then_inc(pv_taken, 1)

            for n in range(STEPS):
                for hh in range(GH):
                    i = CTX_CHUNKS + GH * n + hh
                    sc.wait_ge(score_ready, i + 1)
                    if n >= 2 and hh == 0:
                        sc.wait_ge(pv_done, n - 1)
                    nc.scalar.activation(probs[:, n % 2, hh, :], score_bank(i), ACT.Exp, scale=SCALE).then_inc(score_done, 1)
                if n and n % KB == 0:
                    take_pv(n // KB - 1)
            take_pv(UNITS - 1)

            def high(k):
                rows = FR if k % XJ == FB else P
                sc.wait_ge(xa_hid, k + 1)
                if k >= 4:
                    sc.wait_ge(xa_summed, k - 3)
                nc.scalar.copy(hid_hi[0:rows, k % 4, :], hid[0:rows, k % 3, :]).then_inc(xa_high, 1)

            def take_acc(th):
                sc.wait_ge(xa_summed, XJ * (th + 1))
                nc.scalar.copy(acc_T[:, th, :], acc_banks[th]).then_inc(acc_taken, 1)

            def router_exp(th):
                sc.wait_ge(shifted, th + 1)
                nc.scalar.activation(router[:, 1, :, :], router[:, 0, :, :], ACT.Exp).then_inc(exp_ready, 1)

            for k in range(XA):
                rows = FR if k % XJ == FB else P
                sc.wait_ge(xa_ready, k + 1)
                if k >= 2:
                    sc.wait_ge(xa_hid, k - 1)
                nc.scalar.activation(gelu[0:rows, k % 2, :], score_bank(k)[0:rows, :], ACT.Gelu_apprx_tanh).then_inc(xa_gelu, 1)
                if k:
                    high(k - 1)
                w = weight_chunk_at(k)
                if w is not None:
                    sc.wait_ge(wt_ready, w + 1)
                    if w < NE:
                        nc.scalar.copy(w13_T_hi[:, 512 * w:512 * (w + 1)], weight_bank)
                        if w >= 2:
                            sc.wait_ge(wt_split, w - 1)
                        nc.scalar.copy(stage[:, w % 2, :], weight_bank).then_inc(wt_taken, 1)
                    else:
                        nc.scalar.copy(w2_T[:, 512 * (w - NE):512 * (w - NE + 1)], weight_bank).then_inc(wt_taken, 1)
                if k == ACC:
                    take_acc(0)
                if k == ACC + 14:
                    router_exp(0)
            high(XA - 1)
            take_acc(1)

            for u in range(4 * NE):
                sc.wait_ge(gate_ready, u + 1)
                if u >= 3:
                    sc.wait_ge(moe_act, u - 2)
                nc.scalar.activation(silu[:, u % 3, :], gate_up_banks[u % 2][:, 0, :], ACT.Silu).then_inc(moe_silu, 1)
                if u == 11:
                    router_exp(1)

        @block.tensor
        def _(pe):
            mm = nc.tensor.matmul
            jobs = [0]

            def vec_slot():
                n = jobs[0]
                jobs[0] += 1
                if n >= 2:
                    pe.wait_ge(vec_free, n - 1)
                return pair_of_banks(n)

            def half_transposes(slot, src, th):
                for b in range(HB):
                    last = nc.tensor.transpose(slot[:, P * b:P * (b + 1)], src[:, HB * th + b, :], ident[:, :])
                last.then_inc(vec_ready, 1)

            pe.wait_ge(ident_made, 1)
            pe.wait_ge(x_here, 16)
            slot = vec_slot()
            for tb in range(TB):
                last = nc.tensor.transpose(slot[:, P * tb:P * (tb + 1)], x_rows[:, tb, :], ident[:, :])
            last.then_inc(vec_ready, 1)

            pe.wait_ge(vec_free, 1)
            pe.wait_ge(x_T_half, 1)
            pe.wait_ge(wqkv_here, 48)
            for w in (1, 0):
                slot = vec_slot()
                for th in range(2):
                    hs = slice(HALF * th, HALF * (th + 1))
                    last = mm(slot[:, hs], wqkv[:, C * w:C * (w + 1)], x_T[:, hs], start=True, stop=True)
                last.then_inc(vec_ready, 1)
            slot = vec_slot()
            for tb in range(TB):
                last = mm(slot[:, P * tb:P * (tb + 1)], x_T[:, P * tb:P * (tb + 1)], wqkv[:, 2 * C:3 * C], start=True, stop=True)
            last.then_inc(vec_ready, 1)

            def context_transposes(c):
                blocks, _, _ = context_chunk(c)
                loads = {min(j, FB - 1) // (FB // CTX_LOADS) for j in blocks}
                for n in sorted(loads):
                    pe.wait_ge(ctx_here[n], 16)
                if blocks[-1] == FB:
                    pe.wait_ge(ctx_rest_here, 16)
                if c >= 3:
                    pe.wait_ge(score_done, c - 2)
                bank = score_bank(c)
                for n, j in enumerate(blocks):
                    if j < FB:
                        last = nc.tensor.transpose(bank[:, P * n:P * (n + 1)], ctx_rows[:, j, :], ident[:, :])
                    else:
                        last = nc.tensor.transpose(bank[:, P * n:P * n + FR], ctx_rest[:, :], ident[0:FR, 0:FR])
                last.then_inc(score_ready, 1)

            def max_tile(t):
                _, h, tb = max_tile_of(t)
                half, b = divmod(tb, HB)
                slot = vec_slot()
                for n in range(2):
                    last = mm(slot[:, HALF * n:HALF * (n + 1)], q_stack[:, half, h, P * b:P * (b + 1)],
                              k_stack[:, h, HALF * n:HALF * (n + 1)], start=True, stop=True)
                last.then_inc(vec_ready, 1)

            def max_rows(u, behind=0):
                slot = vec_slot()
                pe.wait_ge(vec_free, jobs[0] - 1 - behind)
                nc.tensor.transpose(slot[0:UT, 0:P], neg_max[:, u, :], ident[:, :]).then_inc(vec_ready, 1)

            def attend_rows(u):
                slot = vec_slot()
                pe.wait_ge(pv_taken, u + 1)
                for b in range(HB):
                    last = nc.tensor.transpose(slot[:, P * b:P * (b + 1)], o_T[:, u % 2, P * b:P * (b + 1)], ident[:, :])
                last.then_inc(vec_ready, 1)

            def scores(n, hh):
                u, kb = divmod(n, KB)
                half, g = divmod(u, NG)
                i = CTX_CHUNKS + GH * n + hh
                h = GH * g + hh
                pe.wait_ge(score_done, i - 2)
                mm(score_bank(i), k_stack[:, h, P * kb:P * (kb + 1)], q_stack[:, half, h, :],
                   start=True, stop=True).then_inc(score_ready, 1)

            def weighted_sums(n):
                u, kb = divmod(n, KB)
                g = u % NG
                if kb == 0 and n:
                    pe.wait_ge(pv_taken, u)
                pe.wait_ge(score_done, CTX_CHUNKS + GH * (n + 1))
                for hh in range(GH):
                    last = mm(pv_bank[VW * hh:VW * (hh + 1), :], v_strip[:, kb, GH * g + hh, :], probs[:, n % 2, hh, :],
                              start=(kb == 0), stop=(kb == KB - 1))
                last.then_inc(pv_done, 1)

            def attended_T(th):
                slot = vec_slot()
                pe.wait_ge(vec_free, jobs[0] - 1)
                half_transposes(slot, att_rows, th)

            def project(th):
                slot = vec_slot()
                pe.wait_ge(vec_free, jobs[0] - 1)
                pe.wait_ge(proj_here, 48)
                for b in range(HB):
                    last = mm(slot[:, C * b:C * (b + 1)], att_T[:, P * b:P * (b + 1)], wproj[:, :], start=True, stop=True)
                last.then_inc(vec_ready, 1)

            def rows_to_T(th, norms):
                slot = vec_slot()
                pe.wait_ge(normed, norms)
                half_transposes(slot, x_rows, th)

            for c in range(CTX_EARLY):
                context_transposes(c)
            pe.wait_ge(stacked[0], 16 * (1 + PARTS))
            for t in range(UT + LEAD):
                if t == UT:
                    max_rows(0)
                    pe.wait_ge(stacked[1], 16 * (1 + PARTS))
                max_tile(t)
                c = CTX_EARLY + t // 2
                if t % 2 == 1 and c < CTX_CHUNKS:
                    context_transposes(c)

            for n in range(STEPS):
                u, kb = divmod(n, KB)
                if kb == 0:
                    pe.wait_ge(m_rows, 16 * PARTS * (u + 1))
                if kb == 2 and u:
                    attend_rows(u - 1)
                if n == 20:
                    pe.wait_ge(stacked[2], 16 * PARTS)
                if n == PROJ[0]:
                    attended_T(0)
                if n == PROJ[0] + 1:
                    project(0)
                if n == PROJ[0] + 6:
                    rows_to_T(0, 1)
                    x1_jobs = [jobs[0]]
                tiles = iter(max_tiles_at(n))
                for hh in range(GH):
                    scores(n, hh)
                    if hh == 2 and n:
                        weighted_sums(n - 1)
                    if hh < 2:
                        for t in tiles:
                            max_tile(t)
                            break
                    if hh == 0 and kb == KB - 2 and u + 1 < UNITS:
                        max_rows(u + 1, behind=len(max_tiles_at(n)[0:1]))
            weighted_sums(STEPS - 1)

            def cross(k):
                th, j = divmod(k, XJ)
                rows = FR if j == FB else P
                if j == 0:
                    pe.wait_ge(vec_free, x1_jobs[th])
                if k >= 3:
                    pe.wait_ge(xa_hid, k - 2)
                bank = score_bank(k)[0:rows, :]
                cs = slice(P * j, P * j + rows)
                mm(bank, ctx_T_hi[:, cs], x1_T_hi[th][:, :], start=True, stop=False)
                mm(bank, ctx_T_hi[:, cs], x1_T_lo[th][:, :], start=False, stop=False)
                mm(bank, ctx_T_lo[:, cs], x1_T_hi[th][:, :], start=False, stop=True).then_inc(xa_ready, 1)

            def cross_sum(k):
                th, j = divmod(k, XJ)
                c = chunk_of(k)
                rows = FR if j == FB else P
                if j % 4 == 0:
                    pe.wait_ge(ctx_low, c + 1)
                pe.wait_ge(xa_low[k % 2], k // 2 + 1)
                cs = slice(C * (j % 4), C * (j % 4 + 1))
                hi, lo = ctx_hi[0:rows, c % 2, cs], ctx_lo[0:rows, c % 2, cs]
                mm(acc_banks[th], hi, hid_hi[0:rows, k % 4, :], start=(j == 0), stop=False)
                mm(acc_banks[th], lo, hid_hi[0:rows, k % 4, :], start=False, stop=False)
                mm(acc_banks[th], hi, hid_lo[0:rows, k % 4, :], start=False, stop=(j == FB)).then_inc(xa_summed, 1)

            def weight_transposes(w):
                if w == 0:
                    pe.wait_ge(experts_here, 32)
                else:
                    pe.wait_ge(wt_taken, w)
                for n in range(4):
                    if w < NE:
                        src = w13_rows[:, 4 * w + n, :]
                    else:
                        src = w2_rows[:, 2 * (w - NE) + n // 2, P * (n % 2):P * (n % 2 + 1)]
                    last = nc.tensor.transpose(weight_bank[:, P * n:P * (n + 1)], src, ident[:, :])
                last.then_inc(wt_ready, 1)

            def crossed_rows(th):
                slot = vec_slot()
                pe.wait_ge(acc_taken, th + 1)
                for b in range(HB):
                    last = nc.tensor.transpose(slot[:, P * b:P * (b + 1)], acc_T[:, th, P * b:P * (b + 1)], ident[:, :])
                last.then_inc(vec_ready, 1)

            def router_logits(th):
                slot = vec_slot()
                pe.wait_ge(x2_split, th + 1)
                for b in range(HB):
                    last = mm(slot[:, NE * b:NE * (b + 1)], x2_T[:, th, P * b:P * (b + 1)], gate_T[:, :], start=True, stop=True)
                last.then_inc(vec_ready, 1)

            pe.wait_ge(ctx_split, CTX_CHUNKS)
            pe.wait_ge(score_done, CTX_CHUNKS + GH * STEPS)
            for k in range(XA + LAG):
                if k < XA:
                    cross(k)
                if k == 1:
                    attend_rows(UNITS - 1)
                if k == LAG:
                    pe.wait_ge(pv_taken, UNITS)
                if k == PROJ[1]:
                    attended_T(1)
                if k == PROJ[1] + 2:
                    project(1)
                if k == PROJ[1] + 9:
                    rows_to_T(1, 2)
                    x1_jobs.append(jobs[0])
                w = weight_chunk_at(k)
                if w is not None:
                    weight_transposes(w)
                if k == ACC + 2:
                    crossed_rows(0)
                if k == ACC + 9:
                    rows_to_T(0, 3)
                if k == ACC + 12:
                    router_logits(0)
                if k >= LAG:
                    cross_sum(k - LAG)

            def gate_up(u):
                m, ib = divmod(u, 2)
                th, e = divmod(m, NE)
                for n, (ready, read) in enumerate(((gate_ready, moe_silu), (up_ready, moe_act))):
                    if u >= 2:
                        pe.wait_ge(read, u - 1)
                    col = 2 * INTER * e + INTER * n + P * ib
                    hi, lo = w13_T_hi[:, col:col + P], w13_T_lo[:, col:col + P]
                    bank = gate_up_banks[u % 2][:, n, :]
                    mm(bank, hi, x2_T_hi[:, th, :], start=True, stop=False)
                    mm(bank, hi, x2_T_lo[:, th, :], start=False, stop=False)
                    mm(bank, lo, x2_T_hi[:, th, :], start=False, stop=True).then_inc(ready, 1)

            def down(m):
                e = m % NE
                pe.wait_ge(moe_act, 2 * m + 2)
                if m == 1:
                    pe.wait_ge(acc_taken, 2)
                if m >= 2:
                    pe.wait_ge(down_taken, m - 1)
                for b in range(HB):
                    for ib in range(2):
                        last = mm(down_banks[m % 2][:, C * b:C * (b + 1)], act[:, 2 * (m % 2) + ib, P * b:P * (b + 1)],
                                  w2_T[:, (2 * e + ib) * C:(2 * e + ib + 1) * C], start=(ib == 0), stop=(ib == 1))
                last.then_inc(down_ready, 1)

            pe.wait_ge(wt_split, NE)
            pe.wait_ge(wt_taken, WT_CHUNKS)
            for m in range(2 * NE):
                if m == NE:
                    pe.wait_ge(x2_split, 2)
                gate_up(2 * m)
                gate_up(2 * m + 1)
                if m == 0:
                    crossed_rows(1)
                if m:
                    down(m - 1)
                if m == 3:
                    rows_to_T(1, 4)
                if m == 4:
                    router_logits(1)
            down(2 * NE - 1)

        @block.vector
        def _(ve):
            V = nc.vector
            links, jobs = [0], [0]

            def link(ins):
                links[0] += 1
                ins.then_inc(chain, 1)
                ve.wait_ge(chain, links[0])

            def vec_slot():
                n = jobs[0]
                jobs[0] += 1
                ve.wait_ge(vec_ready, n + 1)
                return pair_of_banks(n)

            link(V.memset(v_strip[:, :, :, :], 0.0))
            V.memset(v_strip[:, :, :, D:D + 1], 1.0).then_inc(strips_set, 1)

            slot = vec_slot()
            V.tensor_copy(x_T[:, 0:HALF], slot[:, 0:HALF]).then_inc(vec_free, 1)

            ve.wait_ge(wqkv_here, 48)
            for parts, made, left, w in ((k_parts, k_made, k_rest[:, :], 1), (q_parts, q_made, q_rest, 0)):
                slot = vec_slot()
                ve.wait_ge(made, 1)
                V.scalar_tensor_tensor(out=left, in0=slot, scalar=bias_col[:, w:w + 1], in1=parts[:, 0, :],
                                       op0=ALU.add, op1=ALU.subtract).then_inc(vec_free, 1)
            for parts, made, left in ((k_parts, k_made, k_rest[:, :]), (q_parts, q_made, q_rest)):
                ve.wait_ge(made, 2)
                V.tensor_tensor(parts[:, 2, :], left, parts[:, 1, :], ALU.subtract).then_inc(made, 1)

            slot = vec_slot()
            ve.wait_ge(strips_set, 1)
            for kb in range(KB):
                last = V.tensor_tensor(v_strip[:, kb, :, 0:D], slot[:, C * kb:C * (kb + 1)].rearrange("p (h d) -> p h d", d=D),
                                       bias_v[:, :].rearrange("p (h d) -> p h d", d=D), ALU.add)
            last.then_inc(vec_free, 1)

            def row_max(t):
                slot = vec_slot()
                u, i = divmod(t, UT)
                V.tensor_reduce(neg_max[:, u, i:i + 1], slot, axis=AX.X, op=ALU.max, negate=True).then_inc(vec_free, 1)

            def split_max(u):
                slot = vec_slot()
                src = slot[0:UT, 0:P]
                if u >= 2:
                    ve.wait_ge(m_rows, 16 * PARTS * (u - 1))
                link(V.tensor_copy(m_parts[:, u % 2, 0, :], src))
                V.tensor_tensor(m_rest[:, u % 2, :], src, m_parts[:, u % 2, 0, :], ALU.subtract).then_inc(vec_free, 1)
                ve.wait_ge(vec_free, jobs[0])
                link(V.tensor_copy(m_parts[:, u % 2, 1, :], m_rest[:, u % 2, :]))
                V.tensor_tensor(m_parts[:, u % 2, 2, :], m_rest[:, u % 2, :], m_parts[:, u % 2, 1, :],
                                ALU.subtract).then_inc(m_made, 1)

            def divide(u):
                half, g = divmod(u, NG)
                slot = vec_slot()
                sums = slot[:, 0:HALF].rearrange("p (s w) -> p s w", w=VW)
                V.reciprocal(recip[:, u % 2, :].unsqueeze(2), sums[:, :, D:D + 1]).then_inc(o_read, 1)
                ve.wait_ge(o_read, u + 1)
                dst = att_rows[:, HB * half:HB * (half + 1), GH * D * g:GH * D * (g + 1)]
                over = recip[:, u % 2, :].rearrange("p (b h) -> p b h", h=GH).unsqueeze(3).broadcast_to([P, HB, GH, D])
                V.tensor_tensor(dst.rearrange("p b (h d) -> p b h d", d=D), sums[:, :, 0:D].rearrange("p (b h) d -> p b h d", h=GH),
                                over, ALU.mult).then_inc(vec_free, 1)

            def flat(rows, th):
                return rows[:, HB * th:HB * (th + 1), :].rearrange("p t c -> p (t c)")

            def norm_stats(th):
                for b in range(HB):
                    last = V.bn_stats(stats[:, b, :], pre_norm[:, HB * th + b, :])
                link(last)
                for b in range(HB):
                    last = V.bn_aggr(mean_var[:, b, :], stats[:, b, :])
                link(last)

            def norm_root():
                var, r, t, t2 = (norm_s[:, i, :] for i in range(4))
                link(V.tensor_scalar(var, mean_var[:, :, 1], EPS, None, ALU.add))
                link(V.tensor_scalar(r.bitcast(i32), var.bitcast(i32), -0.5, float(0x5F3759DF), ALU.mult, ALU.add))
                for _ in range(3):
                    link(V.scalar_tensor_tensor(out=t, in0=r, scalar=-0.5, in1=r, op0=ALU.mult, op1=ALU.mult))
                    link(V.tensor_tensor(t2, t, var, ALU.mult))
                    link(V.scalar_tensor_tensor(out=r, in0=t2, scalar=1.5, in1=r, op0=ALU.add, op1=ALU.mult))

            def norm_apply(th):
                for b in range(HB):
                    tb = HB * th + b
                    last = V.tensor_scalar(x_rows[:, tb, :], pre_norm[:, tb, :], mean_var[:, b, 0:1], norm_s[:, 1, b:b + 1],
                                           ALU.subtract, ALU.mult)
                last.then_inc(normed, 1)

            def take_attended():
                slot = vec_slot()
                V.tensor_copy(att_T[:, :], slot[:, 0:HALF]).then_inc(vec_free, 1)

            def add_projected(th):
                slot = vec_slot()
                ve.wait_ge(pre_bias, 1)
                V.tensor_tensor(flat(pre_norm, th), slot[:, 0:HALF], flat(pre_norm, th), ALU.add).then_inc(vec_free, 1)
                ve.wait_ge(vec_free, jobs[0])

            def split_x1(th):
                slot = vec_slot()
                link(V.tensor_copy(x1_T_hi[th][:, :], slot[:, 0:HALF]))
                V.tensor_tensor(x1_T_lo[th][:, :], slot[:, 0:HALF], x1_T_hi[th][:, :].bitcast(f32), ALU.subtract).then_inc(vec_free, 1)

            for t in range(UT):
                row_max(t)
            split_max(0)
            for t in range(UT, UT + LEAD):
                row_max(t)
            for n in range(STEPS):
                u, kb = divmod(n, KB)
                if kb == 2 and u:
                    divide(u - 1)
                if n == PROJ[0]:
                    take_attended()
                if n == PROJ[0] + 1:
                    add_projected(0)
                    norm_stats(0)
                if n == PROJ[0] + 3:
                    norm_root()
                if n == PROJ[0] + 4:
                    norm_apply(0)
                if n == PROJ[0] + 6:
                    split_x1(0)
                tiles = max_tiles_at(n)
                for t in tiles[0:1]:
                    row_max(t)
                if kb == KB - 2 and u + 1 < UNITS:
                    split_max(u + 1)
                for t in tiles[1:]:
                    row_max(t)

            def add_crossed(th):
                slot = vec_slot()
                V.tensor_tensor(flat(pre_norm, th), slot[:, 0:HALF], flat(x_rows, th), ALU.add).then_inc(vec_free, 1)
                ve.wait_ge(vec_free, jobs[0])

            def split_x2(th):
                slot = vec_slot()
                V.tensor_copy(x2_T[:, th, :], slot[:, 0:HALF]).then_inc(vec_free, 1)
                ve.wait_ge(vec_free, jobs[0])
                link(V.tensor_copy(x2_T_hi[:, th, :], x2_T[:, th, :]))
                V.tensor_tensor(x2_T_lo[:, th, :], x2_T[:, th, :], x2_T_hi[:, th, :].bitcast(f32), ALU.subtract).then_inc(x2_split, 1)

            def over_e(a):
                return a.unsqueeze(2).broadcast_to([P, HB, NE])

            sh, ex, sc, masked, sel, wt = (router[:, i, :, :] for i in range(6))
            groups, rank4, rank8 = router[:, 6, :, 0:4], router[:, 6, :, 4:8], router[:, 7, :, :]

            def route_shift():
                slot = vec_slot()
                V.tensor_copy(logits[:, :, :], slot[:, 0:HB * NE].rearrange("p (t e) -> p t e", e=NE)).then_inc(vec_free, 1)
                ve.wait_ge(vec_free, jobs[0])
                link(V.tensor_reduce(small[:, 0, :], logits[:, :, :], axis=AX.X, op=ALU.max))
                V.tensor_tensor(sh, logits[:, :, :], over_e(small[:, 0, :]), ALU.subtract).then_inc(shifted, 1)

            def rank(dst, val, lt, n):
                gt = pair[:, 0, 0:HB * n * n].rearrange("p (t j i) -> p t j i", j=n, i=n)
                ge = pair[:, 1, 0:HB * n * n].rearrange("p (t j i) -> p t j i", j=n, i=n)
                vi = val.unsqueeze(2).broadcast_to([P, HB, n, n])
                vj = val.unsqueeze(3).broadcast_to([P, HB, n, n])
                V.tensor_tensor(gt, vi, vj, ALU.is_gt)
                link(V.tensor_tensor(ge, vi, vj, ALU.is_ge))
                link(V.tensor_tensor(ge, ge, lt.unsqueeze(1).broadcast_to([P, HB, n, n]), ALU.mult))
                link(V.tensor_tensor(gt, gt, ge, ALU.max))
                link(V.tensor_reduce(dst, gt, axis=AX.X, op=ALU.add))

            def route_groups(th):
                ve.wait_ge(exp_ready, th + 1)
                link(V.tensor_reduce(small[:, 1, :], ex, axis=AX.X, op=ALU.add))
                link(V.reciprocal(small[:, 2, :], small[:, 1, :]))
                link(V.tensor_tensor(sc, ex, over_e(small[:, 2, :]), ALU.mult))
                link(V.tensor_tensor(groups, sc[:, :, 0::2], sc[:, :, 1::2], ALU.max))
                ve.wait_ge(masks_made, 2)
                rank(rank4, groups, lt4[:, :, :], 4)
                link(V.tensor_scalar(groups, rank4, 2.0, None, ALU.is_lt))
                link(V.tensor_tensor(masked.rearrange("p t (g o) -> p t g o", o=2), sc.rearrange("p t (g o) -> p t g o", o=2),
                                     groups.unsqueeze(3).broadcast_to([P, HB, 4, 2]), ALU.mult))

            def route_experts(th):
                rank(rank8, masked, lt8[:, :, :], NE)
                link(V.tensor_scalar(sel, rank8, 2.0, None, ALU.is_lt))
                link(V.tensor_tensor(wt, masked, sel, ALU.mult))
                link(V.tensor_reduce(small[:, 3, :], wt, axis=AX.X, op=ALU.add))
                link(V.reciprocal(small[:, 0, :], small[:, 3, :]))
                link(V.tensor_tensor(combine[:, HB * th:HB * (th + 1), :], wt, over_e(small[:, 0, :]), ALU.mult))

            def high_rows(c):
                blocks, _, _ = context_chunk(c % CTX_CHUNKS)
                whole = [b for b in blocks if b < FB]
                rows = ctx_rows[:, whole[0]:whole[-1] + 1, :].rearrange("p j c -> p (j c)")
                if c >= 2:
                    ve.wait_ge(xa_summed, first_tile_of(c - 1))
                copy = V.tensor_copy(ctx_hi[:, c % 2, 0:C * len(whole)], rows)
                if blocks[-1] == FB:
                    at = C * len(whole)
                    copy = V.tensor_copy(ctx_hi[0:FR, c % 2, at:at + C], ctx_rest[:, :])
                copy.then_inc(ctx_high, 1)

            def low(k):
                rows = FR if k % XJ == FB else P
                ve.wait_ge(xa_high, k + 1)
                V.tensor_tensor(hid_lo[0:rows, k % 4, :], hid[0:rows, k % 3, :], hid_hi[0:rows, k % 4, :].bitcast(f32),
                                ALU.subtract).then_inc(xa_low[0], 1)

            ve.wait_ge(pv_done, STEPS)
            high_rows(0)
            for k in range(XA):
                rows = FR if k % XJ == FB else P
                ve.wait_ge(xa_gelu, k + 1)
                if k >= 3:
                    ve.wait_ge(xa_low[(k - 3) % 2], (k - 3) // 2 + 1)
                V.tensor_tensor(hid[0:rows, k % 3, :], gelu[0:rows, k % 2, :], score_bank(k)[0:rows, :], ALU.mult).then_inc(xa_hid, 1)
                if k % 2 == 1:
                    low(k - 1)
                if last_of_chunk(k) and k + 1 < XA:
                    high_rows(chunk_of(k) + 1)
                if k == 1:
                    divide(UNITS - 1)
                if k == PROJ[1]:
                    take_attended()
                if k == PROJ[1] + 2:
                    add_projected(1)
                if k == PROJ[1] + 3:
                    norm_stats(1)
                if k == PROJ[1] + 5:
                    norm_root()
                if k == PROJ[1] + 7:
                    norm_apply(1)
                if k == PROJ[1] + 9:
                    split_x1(1)
                if k == ACC + 2:
                    add_crossed(0)
                if k == ACC + 3:
                    norm_stats(0)
                if k == ACC + 5:
                    norm_root()
                if k == ACC + 7:
                    norm_apply(0)
                if k == ACC + 9:
                    split_x2(0)
                if k == ACC + 12:
                    route_shift()
                if k == ACC + 17:
                    route_groups(0)
                if k == ACC + 20:
                    route_experts(0)

            def hidden(u):
                m, ib = divmod(u, 2)
                ve.wait_ge(moe_silu, u + 1)
                ve.wait_ge(up_ready, u + 1)
                if m >= 2:
                    ve.wait_ge(down_ready, m - 1)
                V.tensor_tensor(act[:, 2 * (m % 2) + ib, :], silu[:, u % 3, :], gate_up_banks[u % 2][:, 1, :],
                                ALU.mult).then_inc(moe_act, 1)

            def add_expert(m):
                th, e = divmod(m, NE)
                ve.wait_ge(down_ready, m + 1)
                if e:
                    ve.wait_ge(down_taken, m)
                for b in range(HB):
                    tb = HB * th + b
                    base = pre_norm if e else x_rows
                    last = V.scalar_tensor_tensor(out=pre_norm[:, tb, :], in0=down_banks[m % 2][:, C * b:C * (b + 1)],
                                                  scalar=combine[:, tb, e:e + 1], in1=base[:, tb, :], op0=ALU.mult, op1=ALU.add)
                last.then_inc(down_taken, 1)

            for m in range(2 * NE):
                hidden(2 * m)
                hidden(2 * m + 1)
                if m == 0:
                    add_crossed(1)
                    norm_stats(1)
                if m:
                    add_expert(m - 1)
                if m == 1:
                    norm_root()
                if m == 2:
                    norm_apply(1)
                if m == 3:
                    split_x2(1)
                if m == 4:
                    route_shift()
                if m == 6:
                    route_groups(1)
                if m == 7:
                    route_experts(1)
                if m == NE + 1:
                    ve.wait_ge(down_taken, NE)
                    norm_stats(0)
                if m == NE + 2:
                    norm_root()
                if m == NE + 3:
                    norm_apply(0)
            add_expert(2 * NE - 1)
            ve.wait_ge(down_taken, 2 * NE)
            norm_stats(1)
            norm_root()
            norm_apply(1)


_INS = ['x', 'ctx_1024', 'L0_attn_qkv_w', 'L0_attn_qkv_b', 'L0_attn_proj_w', 'L0_attn_proj_b', 'L0_ffn_gate_w',
        'L0_ffn_w13_weight', 'L0_ffn_w2_weight']


def kernel(**inputs):
    import numpy as _np
    import concourse.bacc as _bacc
    from concourse import mybir as _mybir
    from concourse.bass_utils import run_bass_kernel_spmd as _run

    nc = _bacc.Bacc("TRN2", target_bir_lowering=False, num_devices=1)
    arrays, args = {}, []
    for name in _INS:
        a = _np.ascontiguousarray(inputs[name])
        arrays[f"in_{name}"] = a
        args.append(nc.dram_tensor(f"in_{name}", a.shape, _mybir.dt.from_np(a.dtype), kind="ExternalInput").ap())
    args.append(nc.dram_tensor("out_0", (1, N, C), _mybir.dt.float32, kind="ExternalOutput").ap())
    args.append(nc.dram_tensor("kept_k", (PARTS, D, H, N), _mybir.dt.bfloat16, kind="Internal").ap())
    args.append(nc.dram_tensor("kept_q", (2, PARTS, D, H, HALF), _mybir.dt.bfloat16, kind="Internal").ap())
    build(nc, *args)
    r = _run(nc, [arrays], core_ids=[0])
    return r.results[0]["out_0"]
```

```python
import concourse.bass as bass
from concourse import mybir
from contextlib import ExitStack


P = 128
N = 1024
C = 128
H = 16
D = C // H
F = 6404
NE = 8
INTER = 256
TB = N // P
HALF = N // 2
HB = TB // 2
EPS = 1e-5
SCALE = float(D) ** -0.5

PARTS = 3
PAIRS = PARTS * D
MROW = PARTS * PAIRS
ONES = 0x3F803F80
GH = 4
NG = H // GH
VW = 32
KB = N // P
UNITS = 2 * NG
STEPS = UNITS * KB
UT = GH * HB
LEAD = 4
MAX_TILES = UNITS * UT
MAX_STEPS = STEPS - UT // 2

FB = F // P
FR = F - FB * P
CTX_CHUNKS = -(-(FB + 1) // 4)
CTX_EARLY = 5
ROWS_EARLY = 8
FOUR_FROM = CTX_CHUNKS + GH * MAX_STEPS
SCORE_TILES = CTX_CHUNKS + GH * STEPS
CTX_LOADS = 5
XJ = FB + 1
XA = 2 * XJ
WARM_UP = 6
NEWTON = 3
LAG = 4
WT_CHUNKS = NE + NE // 2

PROJ = (56, 9)
ACC = XJ + LAG
WT_FIRST, WT_EVERY = 14, 5


def max_tiles_at(n):
    first = UT + LEAD + 2 * n
    return range(min(first, MAX_TILES), min(first + 2, MAX_TILES))


def max_tile_of(t):
    u, i = divmod(t, UT)
    half, g = divmod(u, NG)
    return u, GH * g + i // HB, HB * half + i % HB


def context_chunk(c):
    blocks = range(4 * c, min(4 * c + 4, FB + 1))
    return blocks, 4 * c * P, min(4 * P, F - 4 * c * P)


def row_chunk_at(k):
    c = ROWS_EARLY + k // 4
    return c if c < CTX_CHUNKS else None


def weight_chunk_at(k):
    w = (k - WT_FIRST) // WT_EVERY
    return w if k >= WT_FIRST and (k - WT_FIRST) % WT_EVERY == 0 and w < WT_CHUNKS else None


def build(nc, x, ctx, qkv_w, qkv_b, proj_w, proj_b, gate_w, w13, w2, out, kept_k, kept_q):
    f32 = mybir.dt.float32
    f32r = mybir.dt.float32r
    bf16 = mybir.dt.bfloat16
    u32 = mybir.dt.uint32
    i32 = mybir.dt.int32
    ALU = mybir.AluOpType
    ACT = mybir.ActivationFunctionType
    AX = mybir.AxisListType

    stack = ExitStack()
    with stack:
        def sb(name, shape, dt, scope=stack):
            return scope.enter_context(nc.sbuf_tensor(name, shape, dt))

        def sem(name):
            return stack.enter_context(nc.semaphore(name))

        ident = sb("ident", [P, P], f32)
        x_rows = sb("x_rows", [P, TB, C], f32)
        pre_norm = sb("pre_norm", [P, TB, C], f32)
        gate_T = sb("gate_T", [P, NE], f32)
        lt4 = sb("lt4", [P, 4, 4], f32)
        lt8 = sb("lt8", [P, NE, NE], f32)
        stats = sb("stats", [P, HB, 6], f32)
        mean_var = sb("mean_var", [P, HB, 2], f32)
        norm_s = sb("norm_s", [P, 4, HB], f32)
        whole = ExitStack()
        ctx_rows = sb("ctx_rows", [P, FB, C], f32, whole)
        ctx_rest = sb("ctx_rest", [FR, C], f32, whole)
        whole.close()
        ctx_lo = sb("ctx_lo", [P, FB, C], f32r)
        rest_lo = sb("rest_lo", [FR, C], f32r)
        ctx_T_hi = sb("ctx_T_hi", [P, F], f32r)
        unsplit = ExitStack()
        ctx_T = sb("ctx_T", [P, F], f32, unsplit)
        unsplit.close()
        ctx_T_lo = sb("ctx_T_lo", [P, F], f32r)
        acc_T = sb("acc_T", [P, 2, HALF], f32)
        recip = sb("recip", [P, 2, HB * GH], f32)
        first = ExitStack()
        x1a_T_hi = sb("x1a_T_hi", [P, HALF], f32r, first)
        x1a_T_lo = sb("x1a_T_lo", [P, HALF], f32r, first)
        first.close()
        x2_T = sb("x2_T", [P, 2, HALF], f32)

        att = ExitStack()
        q_stack = sb("q_stack", [P, 2, H, HALF], bf16, att)
        k_stack = sb("k_stack", [P, H, N], bf16, att)
        v_strip = sb("v_strip", [P, KB, H, VW], f32, att)
        att_rows = sb("att_rows", [P, TB, C], f32, att)
        att_T = sb("att_T", [P, HALF], f32, att)
        wqkv = sb("wqkv", [P, 3 * C], f32, att)
        bias_col = sb("bias_col", [P, 2], f32, att)
        bias_v = sb("bias_v", [P, C], f32, att)
        wproj = sb("wproj", [P, C], f32, att)
        bias_p = sb("bias_p", [P, C], f32, att)
        neg_max = sb("neg_max", [P, UNITS, UT], f32, att)
        m_parts = sb("m_parts", [UT, 2, PARTS, P], bf16, att)
        m_rest = sb("m_rest", [UT, 2, P], f32, att)
        pre = ExitStack()
        x_T = sb("x_T", [P, N], f32, pre)
        q_parts = sb("q_parts", [P, PARTS, N], bf16, pre)
        k_parts = sb("k_parts", [P, PARTS, N], bf16, pre)
        k_rest = sb("k_rest", [P, N], f32, pre)
        q_rest = att_rows[:, :, :].rearrange("p t c -> p (t c)")
        halves = (slice(0, HALF), slice(HALF, N))
        pre.close()
        probs = sb("probs", [P, 2, GH, HALF], f32, att)
        o_T = sb("o_T", [P, 2, HALF], f32, att)
        att.close()

        cross_only = ExitStack()
        ctx_hi = sb("ctx_hi", [P, FB + 1, C], f32r, cross_only)
        gelu = sb("gelu", [P, 2, HALF], f32, cross_only)
        hid = sb("hid", [P, 3, HALF], f32, cross_only)
        hid_hi = sb("hid_hi", [P, 4, HALF], f32r, cross_only)
        hid_lo = sb("hid_lo", [P, 4, HALF], f32r, cross_only)
        cross_only.close()
        experts_only = ExitStack()
        silu = sb("silu", [P, 3, HALF], f32, experts_only)
        act = sb("act", [P, 4, HALF], f32, experts_only)
        room = sb("room", [P, (FB + 1) * C + 6 * HALF], f32, experts_only)
        w13_T_hi = sb("w13_T_hi", [P, NE * 2 * INTER], f32r, experts_only)
        w13_T_lo = sb("w13_T_lo", [P, NE * 2 * INTER], f32r, experts_only)
        w2_T = sb("w2_T", [P, NE * 2 * C], f32, experts_only)
        x1b_T_hi = sb("x1b_T_hi", [P, HALF], f32r, experts_only)
        x1b_T_lo = sb("x1b_T_lo", [P, HALF], f32r, experts_only)
        router = sb("router", [P, 8, HB, NE], f32, experts_only)
        pair = sb("pair", [P, 2, HB * NE * NE], f32, experts_only)
        small = sb("small", [P, 4, HB], f32, experts_only)
        logits = sb("logits", [P, HB, NE], f32, experts_only)
        combine = sb("combine", [P, TB, NE], f32, experts_only)
        rows_only = ExitStack()
        w13_rows_a = sb("w13_rows_a", [P, 2 * NE, C], f32, rows_only)
        rows_a_end = ExitStack()
        w13_rows_b = sb("w13_rows_b", [P, 2 * NE, C], f32, rows_a_end)
        rows_a_end.close()
        x2_T_hi = sb("x2_T_hi", [P, 2, HALF], f32r, rows_only)
        x2_T_lo = sb("x2_T_lo", [P, 2, HALF], f32r, rows_only)
        rows_only.close()
        w2_rows = sb("w2_rows", [P, NE, INTER], f32, experts_only)
        experts_only.close()
        x1_T_hi = (x1a_T_hi, x1b_T_hi)
        x1_T_lo = (x1a_T_lo, x1b_T_lo)

        psum = stack.enter_context(nc.psum_tensor("psum", [P, 8, 512], f32))

        def pair_of_banks(n):
            b = 2 * (n % 2)
            return psum[:, b:b + 2, :].rearrange("p b c -> p (b c)")

        def score_bank(i):
            if i < FOUR_FROM:
                return psum[:, 4 + i % 3, :]
            return psum[:, (4, 5, 6, 1)[(i - FOUR_FROM) % 4], :]

        def cross_bank(k):
            return psum[:, 4 + k % 3, :]

        pv_bank = psum[:, 7, :]
        acc_banks = (psum[:, 7, :], psum[:, 3, :])
        weight_bank = psum[:, 1, :]
        gate_up_banks = (psum[:, 4:6, :], psum[:, 6:8, :])
        down_banks = (psum[:, 1, :], psum[:, 3, :])
        last_banks = [psum[:, 4 + b, 0:C] for b in range(HB)]

        x_here = sem("x_here")
        wqkv_here = sem("wqkv_here")
        proj_here = sem("proj_here")
        ctx_here = [sem(f"ctx_here{n}") for n in range(CTX_LOADS)]
        ctx_rest_here = sem("ctx_rest_here")
        experts_here = [sem(f"experts_here{n}") for n in range(3)]
        ident_made = sem("ident_made")
        strips_set = sem("strips_set")
        masks_made = sem("masks_made")
        pre_bias = sem("pre_bias")
        stack_set = sem("stack_set")
        x_T_half = sem("x_T_half")
        k_made = sem("k_made")
        q_made = [sem(f"q_made{half}") for half in range(2)]
        q_left = sem("q_left")
        k_kept = sem("k_kept")
        q_kept = [sem(f"q_kept{half}") for half in range(2)]
        stacked = [sem(f"stacked{n}") for n in range(3)]
        vec_ready = sem("vec_ready")
        vec_free = sem("vec_free")
        chain = sem("chain")
        pool_chain = sem("pool_chain")
        m_made = sem("m_made")
        m_rows = sem("m_rows")
        score_ready = sem("score_ready")
        score_done = sem("score_done")
        ctx_high = sem("ctx_high")
        ctx_split = sem("ctx_split")
        pv_done = sem("pv_done")
        pv_taken = sem("pv_taken")
        o_read = sem("o_read")
        xa_ready = sem("xa_ready")
        xa_gelu = sem("xa_gelu")
        xa_hid = sem("xa_hid")
        xa_high = sem("xa_high")
        xa_low = (sem("xa_low_even"), sem("xa_low_odd"))
        xa_summed = sem("xa_summed")
        rows_high = sem("rows_high")
        rows_low = sem("rows_low")
        wt_ready = sem("wt_ready")
        wt_taken = sem("wt_taken")
        wt_split = sem("wt_split")
        acc_taken = sem("acc_taken")
        x2_split = sem("x2_split")
        shifted = sem("shifted")
        exp_ready = sem("exp_ready")
        gate_ready = sem("gate_ready")
        up_ready = sem("up_ready")
        moe_silu = sem("moe_silu")
        moe_act = sem("moe_act")
        down_ready = sem("down_ready")
        down_block = sem("down_block")
        down_taken = sem("down_taken")
        last_sum = sem("last_sum")
        normed = sem("normed")
        stored = sem("stored")

        block = stack.enter_context(nc.Block())

        @block.sync
        def _(sp):
            def stack_k(heads, n):
                sp.wait_ge(stack_set, 2 * n + 1)
                sp.wait_ge(k_kept, 16 * PARTS)
                src = kept_k.rearrange("j d h t -> (j d) h t")[:, heads, :].rearrange("r h t -> r (h t)")
                src = src.unsqueeze(0).broadcast_to([PARTS] + list(src.shape))
                sp.dma_start(k_stack[0:MROW, heads, :].rearrange("r h t -> r (h t)"), src).then_inc(stacked[n], 16)

            def stack_q(half, heads, n):
                sp.wait_ge(stack_set, 2 * n + 2 if n < 2 else 5)
                sp.wait_ge(q_kept[half], 16 * PARTS)
                for a in range(PARTS):
                    src = kept_q[half, a][:, heads, :].rearrange("d h t -> d (h t)")
                    src = src.unsqueeze(0).broadcast_to([PARTS] + list(src.shape))
                    sp.dma_start(q_stack[PAIRS * a:PAIRS * (a + 1), half, heads, :].rearrange("r h t -> r (h t)"),
                                 src).then_inc(stacked[n], 16)

            x_view = x[0].rearrange("(t p) c -> p t c", p=P)
            sp.dma_start(x_rows[:, :, :], x_view).then_inc(x_here, 16)
            sp.dma_start(wqkv[:, :], qkv_w).then_inc(wqkv_here, 16)
            sp.dma_start(bias_col[:, :], qkv_b[0:2 * C].rearrange("(j p) -> p j", p=P),
                         allow_slow_non_contiguous=True).then_inc(wqkv_here, 16)
            sp.dma_start(bias_v[:, :], qkv_b[2 * C:3 * C].partition_broadcast(P)).then_inc(wqkv_here, 16)
            ctx_view = ctx[0, 0:FB * P, :].rearrange("(p j) c -> p j c", j=FB)
            per = FB // CTX_LOADS
            for n in range(CTX_LOADS):
                if n == 2:
                    for part in range(PARTS):
                        sp.wait_ge(k_made, part + 1)
                        sp.dma_start(kept_k[part].rearrange("d h t -> h d t"), k_parts[:, part, :]).then_inc(k_kept, 16)
                        sp.wait_ge(q_made[0], part + 1)
                        sp.dma_start(kept_q[0, part].rearrange("d h t -> h d t"),
                                     q_parts[:, part, 0:HALF]).then_inc(q_kept[0], 16)
                    stack_k(slice(0, GH), 0)
                    stack_q(0, slice(0, GH), 0)
                sp.dma_start(ctx_rows[:, n * per:(n + 1) * per, :],
                             ctx_view[:, n * per:(n + 1) * per, :]).then_inc(ctx_here[n], 16)
            for part in range(PARTS):
                sp.wait_ge(q_made[1], part + 1)
                sp.dma_start(kept_q[1, part].rearrange("d h t -> h d t"),
                             q_parts[:, part, HALF:N]).then_inc(q_kept[1], 16)
            sp.wait_ge(q_kept[1], 16 * PARTS)
            stack_k(slice(GH, H), 1)
            stack_q(0, slice(GH, H), 1)
            stack_q(1, slice(0, H), 2)
            sp.dma_start(ctx_rest[:, :], ctx[0, FB * P:F, :]).then_inc(ctx_rest_here, 16)
            sp.dma_start(wproj[:, :], proj_w).then_inc(proj_here, 16)
            sp.dma_start(bias_p[:, :], proj_b.partition_broadcast(P)).then_inc(proj_here, 16)
            sp.dma_start(gate_T[:, :], gate_w.rearrange("e c -> c e"), allow_slow_non_contiguous=True).then_inc(proj_here, 16)

            for u in range(UNITS):
                half, g = divmod(u, NG)
                sp.wait_ge(m_made, u + 1)
                for a in range(PARTS):
                    dst = q_stack[MROW + a:MROW + a + 1, half, GH * g:GH * (g + 1), :]
                    sp.dma_start(dst.rearrange("o h (b q) -> o (h b) q", q=P), m_parts[:, u % 2, a, :]).then_inc(m_rows, 16)

            w13_view = w13.rearrange("e (b p) c -> p (e b) c", p=P)
            sp.wait_ge(pv_done, STEPS)
            sp.dma_start(w13_rows_a[:, :, :], w13_view[:, 0:2 * NE, :]).then_inc(experts_here[0], 16)
            sp.wait_ge(o_read, UNITS)
            sp.dma_start(w13_rows_b[:, :, :], w13_view[:, 2 * NE:4 * NE, :]).then_inc(experts_here[1], 16)
            sp.wait_ge(wt_taken, NE // 2)
            sp.dma_start(w2_rows[:, :, :], w2.rearrange("e c i -> c e i")).then_inc(experts_here[2], 16)

            out_view = out[0].rearrange("(t p) c -> p t c", p=P)
            for th in range(2):
                sp.wait_ge(normed, th + 5)
                sp.dma_start(out_view[:, HB * th:HB * (th + 1), :], x_rows[:, HB * th:HB * (th + 1), :]).then_inc(stored, 16)
            sp.wait_ge(stored, 32)

        @block.gpsimd
        def _(pool):
            links = [0]

            def link(ins):
                links[0] += 1
                ins.then_inc(pool_chain, 1)
                pool.wait_ge(pool_chain, links[0])

            link(nc.gpsimd.memset(ident[:, :], 0.0))
            nc.gpsimd.affine_select(out=ident[:, :], in_=ident[:, :], compare_op=ALU.not_equal, fill=1.0, base=0,
                                    pattern=[[-1, P]], channel_multiplier=1).then_inc(ident_made, 1)
            pool.wait_ge(ident_made, 1)
            first, later = slice(0, GH), slice(GH, H)
            nc.gpsimd.memset(k_stack[64:P, first, :].bitcast(u32), ONES).then_inc(stack_set, 1)
            nc.gpsimd.memset(q_stack[64:P, 0, first, :].bitcast(u32), 0).then_inc(stack_set, 1)
            nc.gpsimd.memset(k_stack[64:P, later, :].bitcast(u32), ONES).then_inc(stack_set, 1)
            nc.gpsimd.memset(q_stack[64:P, 0, later, :].bitcast(u32), 0).then_inc(stack_set, 1)
            nc.gpsimd.memset(q_stack[64:P, 1, :, :].bitcast(u32), 0).then_inc(stack_set, 1)
            pool.wait_ge(stack_set, 5)

            for c in range(CTX_CHUNKS):
                _, col, width = context_chunk(c)
                cols = slice(col, col + width)
                pool.wait_ge(score_done, c + 1)
                nc.gpsimd.tensor_copy(ctx_T_hi[:, cols], ctx_T[:, cols]).then_inc(ctx_high, 1)
                pool.wait_ge(ctx_high, c + 1)
                nc.gpsimd.tensor_tensor(ctx_T_lo[:, cols], ctx_T[:, cols], ctx_T_hi[:, cols].bitcast(f32),
                                        ALU.subtract).then_inc(ctx_split, 1)

            pool.wait_ge(x_here, 16)
            pool.wait_ge(proj_here, 48)
            nc.gpsimd.tensor_tensor(pre_norm[:, :, :], x_rows[:, :, :],
                                    bias_p[:, :].unsqueeze(1).broadcast_to([P, TB, C]), ALU.add).then_inc(pre_bias, 1)
            for mask, n in ((lt4, 4), (lt8, NE)):
                link(nc.gpsimd.memset(mask[:, :, :], 1.0))
                nc.gpsimd.affine_select(out=mask[:, :, :], in_=mask[:, :, :], compare_op=ALU.is_ge, fill=0.0, base=-1,
                                        pattern=[[1, n], [-1, n]], channel_multiplier=0).then_inc(masks_made, 1)

            def high_rows(c):
                blocks, _, _ = context_chunk(c)
                whole = slice(blocks[0], min(blocks[-1] + 1, FB))
                nc.gpsimd.tensor_copy(ctx_hi[:, whole, :], ctx_rows[:, whole, :]).then_inc(rows_high, 1)
                pool.wait_ge(rows_high, c + 1)

            def low_rows(c):
                blocks, _, _ = context_chunk(c)
                whole = slice(blocks[0], min(blocks[-1] + 1, FB))
                low = nc.gpsimd.tensor_tensor(ctx_lo[:, whole, :], ctx_rows[:, whole, :],
                                              ctx_hi[:, whole, :].bitcast(f32), ALU.subtract)
                if blocks[-1] == FB:
                    link(low)
                    link(nc.gpsimd.tensor_copy(ctx_hi[0:FR, FB, :], ctx_rest[:, :]))
                    low = nc.gpsimd.tensor_tensor(rest_lo[:, :], ctx_rest[:, :],
                                                  ctx_hi[0:FR, FB, :].bitcast(f32), ALU.subtract)
                low.then_inc(rows_low, 1)
                pool.wait_ge(rows_low, c + 1)

            pool.wait_ge(score_ready, CTX_CHUNKS + GH * STEPS // 2)
            for c in range(ROWS_EARLY):
                high_rows(c)
                low_rows(c)
            pool.wait_ge(score_ready, SCORE_TILES)

            for k in range(XA):
                if k % 2 == 1:
                    rows = FR if k % XJ == FB else P
                    pool.wait_ge(xa_high, k + 1)
                    nc.gpsimd.tensor_tensor(hid_lo[0:rows, k % 4, :], hid[0:rows, k % 3, :],
                                            hid_hi[0:rows, k % 4, :].bitcast(f32), ALU.subtract).then_inc(xa_low[1], 1)
                    pool.wait_ge(xa_low[1], k // 2 + 1)
                c = row_chunk_at(k)
                if c is not None and k % 4 == 0:
                    high_rows(c)
                if c is not None and k % 4 == 2:
                    low_rows(c)

        @block.scalar
        def _(sc):
            sc.wait_ge(vec_ready, 1)
            nc.scalar.copy(x_T[:, HALF:N], pair_of_banks(0)[:, HALF:N]).then_inc(x_T_half, 1)

            sc.wait_ge(wqkv_here, 48)
            k_slot, q_slot = pair_of_banks(1), pair_of_banks(2)
            sc.wait_ge(vec_ready, 2)
            nc.scalar.activation(k_parts[:, 0, :], k_slot, ACT.Identity, bias=bias_col[:, 1:2]).then_inc(k_made, 1)
            sc.wait_ge(vec_ready, 3)
            nc.scalar.activation(q_parts[:, 0, halves[0]], q_slot[:, halves[0]], ACT.Identity,
                                 bias=bias_col[:, 0:1]).then_inc(q_made[0], 1)
            sc.wait_ge(vec_free, 2)
            nc.scalar.copy(k_parts[:, 1, :], k_rest[:, :]).then_inc(k_made, 1)
            sc.wait_ge(q_left, 1)
            nc.scalar.copy(q_parts[:, 1, halves[0]], q_rest[:, halves[0]]).then_inc(q_made[0], 1)
            nc.scalar.activation(q_parts[:, 0, halves[1]], q_slot[:, halves[1]], ACT.Identity,
                                 bias=bias_col[:, 0:1]).then_inc(q_made[1], 1)
            sc.wait_ge(vec_free, 3)
            nc.scalar.copy(q_parts[:, 1, halves[1]], q_rest[:, halves[1]]).then_inc(q_made[1], 1)

            for c in range(CTX_CHUNKS):
                _, col, width = context_chunk(c)
                sc.wait_ge(score_ready, c + 1)
                nc.scalar.copy(ctx_T[:, col:col + width], score_bank(c)[:, 0:width]).then_inc(score_done, 1)

            def take_pv(u):
                sc.wait_ge(pv_done, KB * (u + 1))
                if u >= 2:
                    sc.wait_ge(o_read, u - 1)
                nc.scalar.copy(o_T[:, u % 2, :], pv_bank).then_inc(pv_taken, 1)

            for n in range(STEPS):
                for hh in range(GH):
                    i = CTX_CHUNKS + GH * n + hh
                    sc.wait_ge(score_ready, i + 1)
                    if n >= 2 and hh == 0:
                        sc.wait_ge(pv_done, n - 1)
                    nc.scalar.activation(probs[:, n % 2, hh, :], score_bank(i), ACT.Exp, scale=SCALE).then_inc(score_done, 1)
                if n and n % KB == 0:
                    take_pv(n // KB - 1)

            def high(k):
                rows = FR if k % XJ == FB else P
                sc.wait_ge(xa_hid, k + 1)
                if k >= 4:
                    sc.wait_ge(xa_summed, k - 3)
                nc.scalar.copy(hid_hi[0:rows, k % 4, :], hid[0:rows, k % 3, :]).then_inc(xa_high, 1)

            def take_acc(th):
                sc.wait_ge(xa_summed, XJ * (th + 1))
                nc.scalar.copy(acc_T[:, th, :], acc_banks[th]).then_inc(acc_taken, 1)

            def router_exp(th):
                sc.wait_ge(shifted, th + 1)
                nc.scalar.activation(router[:, 1, :, :], router[:, 0, :, :], ACT.Exp).then_inc(exp_ready, 1)

            for k in range(XA):
                rows = FR if k % XJ == FB else P
                sc.wait_ge(xa_ready, k + 1)
                if k >= 2:
                    sc.wait_ge(xa_hid, k - 1)
                nc.scalar.activation(gelu[0:rows, k % 2, :], cross_bank(k)[0:rows, :], ACT.Gelu_apprx_tanh).then_inc(xa_gelu, 1)
                if k == 1:
                    take_pv(UNITS - 1)
                if k:
                    high(k - 1)
                w = weight_chunk_at(k)
                if w is not None:
                    sc.wait_ge(wt_ready, w + 1)
                    dst, at = (w13_T_hi, w) if w < NE else (w2_T, w - NE)
                    nc.scalar.copy(dst[:, 512 * at:512 * (at + 1)], weight_bank).then_inc(wt_taken, 1)
                if k == ACC:
                    take_acc(0)
                if k == ACC + 17:
                    router_exp(0)
            high(XA - 1)
            take_acc(1)

            for u in range(4 * NE):
                sc.wait_ge(gate_ready, u + 1)
                if u >= 3:
                    sc.wait_ge(moe_act, u - 2)
                nc.scalar.activation(silu[:, u % 3, :], gate_up_banks[u % 2][:, 0, :], ACT.Silu).then_inc(moe_silu, 1)
                if u == 11:
                    router_exp(1)

        @block.tensor
        def _(pe):
            mm = nc.tensor.matmul
            jobs = [0]

            def vec_slot():
                n = jobs[0]
                jobs[0] += 1
                if n >= 2:
                    pe.wait_ge(vec_free, n - 1)
                return pair_of_banks(n)

            def half_transposes(slot, src, th):
                for b in range(HB):
                    last = nc.tensor.transpose(slot[:, P * b:P * (b + 1)], src[:, HB * th + b, :], ident[:, :])
                last.then_inc(vec_ready, 1)

            pe.wait_ge(ident_made, 1)
            for _ in range(WARM_UP):
                mm(pv_bank[:, 0:P], ident[:, :], ident[:, :], start=True, stop=True)
            pe.wait_ge(x_here, 16)
            slot = vec_slot()
            for tb in range(TB):
                last = nc.tensor.transpose(slot[:, P * tb:P * (tb + 1)], x_rows[:, tb, :], ident[:, :])
            last.then_inc(vec_ready, 1)

            pe.wait_ge(vec_free, 1)
            pe.wait_ge(x_T_half, 1)
            pe.wait_ge(wqkv_here, 48)
            for w in (1, 0):
                slot = vec_slot()
                for th in range(2):
                    hs = slice(HALF * th, HALF * (th + 1))
                    last = mm(slot[:, hs], wqkv[:, C * w:C * (w + 1)], x_T[:, hs], start=True, stop=True)
                last.then_inc(vec_ready, 1)
            slot = vec_slot()
            for tb in range(TB):
                last = mm(slot[:, P * tb:P * (tb + 1)], x_T[:, P * tb:P * (tb + 1)], wqkv[:, 2 * C:3 * C], start=True, stop=True)
            last.then_inc(vec_ready, 1)

            def context_transposes(c):
                blocks, _, _ = context_chunk(c)
                loads = {min(j, FB - 1) // (FB // CTX_LOADS) for j in blocks}
                for n in sorted(loads):
                    pe.wait_ge(ctx_here[n], 16)
                if blocks[-1] == FB:
                    pe.wait_ge(ctx_rest_here, 16)
                if c >= 3:
                    pe.wait_ge(score_done, c - 2)
                bank = score_bank(c)
                for n, j in enumerate(blocks):
                    if j < FB:
                        last = nc.tensor.transpose(bank[:, P * n:P * (n + 1)], ctx_rows[:, j, :], ident[:, :])
                    else:
                        last = nc.tensor.transpose(bank[:, P * n:P * n + FR], ctx_rest[:, :], ident[0:FR, 0:FR])
                last.then_inc(score_ready, 1)

            def max_tile(t):
                _, h, tb = max_tile_of(t)
                half, b = divmod(tb, HB)
                slot = vec_slot()
                for n in range(2):
                    last = mm(slot[:, HALF * n:HALF * (n + 1)], q_stack[:, half, h, P * b:P * (b + 1)],
                              k_stack[:, h, HALF * n:HALF * (n + 1)], start=True, stop=True)
                last.then_inc(vec_ready, 1)

            def max_rows(u, behind=0):
                slot = vec_slot()
                pe.wait_ge(vec_free, jobs[0] - 1 - behind)
                nc.tensor.transpose(slot[0:UT, 0:P], neg_max[:, u, :], ident[:, :]).then_inc(vec_ready, 1)

            def attend_rows(u):
                slot = vec_slot()
                pe.wait_ge(pv_taken, u + 1)
                for b in range(HB):
                    last = nc.tensor.transpose(slot[:, P * b:P * (b + 1)], o_T[:, u % 2, P * b:P * (b + 1)], ident[:, :])
                last.then_inc(vec_ready, 1)

            def scores(n, hh):
                u, kb = divmod(n, KB)
                half, g = divmod(u, NG)
                i = CTX_CHUNKS + GH * n + hh
                h = GH * g + hh
                if i == FOUR_FROM + 3:
                    pe.wait_ge(vec_free, last_max_job)
                else:
                    pe.wait_ge(score_done, i - 2 if i < FOUR_FROM + 3 else i - 3)
                mm(score_bank(i), k_stack[:, h, P * kb:P * (kb + 1)], q_stack[:, half, h, :],
                   start=True, stop=True).then_inc(score_ready, 1)

            def weighted_sums(n):
                u, kb = divmod(n, KB)
                g = u % NG
                if kb == 0 and n:
                    pe.wait_ge(pv_taken, u)
                pe.wait_ge(score_done, CTX_CHUNKS + GH * (n + 1))
                for hh in range(GH):
                    last = mm(pv_bank[VW * hh:VW * (hh + 1), :], v_strip[:, kb, GH * g + hh, :], probs[:, n % 2, hh, :],
                              start=(kb == 0), stop=(kb == KB - 1))
                last.then_inc(pv_done, 1)

            def attended_T(th):
                slot = vec_slot()
                pe.wait_ge(vec_free, jobs[0] - 1)
                half_transposes(slot, att_rows, th)

            def project(th):
                slot = vec_slot()
                pe.wait_ge(vec_free, jobs[0] - 1)
                pe.wait_ge(proj_here, 48)
                for b in range(HB):
                    last = mm(slot[:, C * b:C * (b + 1)], att_T[:, P * b:P * (b + 1)], wproj[:, :], start=True, stop=True)
                last.then_inc(vec_ready, 1)

            def rows_to_T(th, norms):
                slot = vec_slot()
                pe.wait_ge(normed, norms)
                half_transposes(slot, x_rows, th)

            for c in range(CTX_EARLY):
                context_transposes(c)
            pe.wait_ge(stacked[0], 16 * (1 + PARTS))
            for t in range(UT + LEAD):
                if t == UT:
                    max_rows(0)
                    pe.wait_ge(stacked[1], 16 * (1 + PARTS))
                max_tile(t)
                c = CTX_EARLY + t // 2
                if t % 2 == 1 and c < CTX_CHUNKS:
                    context_transposes(c)

            for n in range(STEPS):
                u, kb = divmod(n, KB)
                if kb == 0:
                    pe.wait_ge(m_rows, 16 * PARTS * (u + 1))
                if kb == 2 and u:
                    attend_rows(u - 1)
                if n == 20:
                    pe.wait_ge(stacked[2], 16 * PARTS)
                if n == PROJ[0]:
                    attended_T(0)
                if n == PROJ[0] + 1:
                    project(0)
                if n == PROJ[0] + 6:
                    rows_to_T(0, 1)
                    x1_jobs = [jobs[0]]
                if n == MAX_STEPS:
                    last_max_job = jobs[0]
                tiles = iter(max_tiles_at(n))
                for hh in range(GH):
                    scores(n, hh)
                    if hh == 0 and kb == KB - 2 and u + 1 < UNITS:
                        max_rows(u + 1)
                    if hh == 2 and n:
                        weighted_sums(n - 1)
                    if hh < 2:
                        for t in tiles:
                            max_tile(t)
                            break

            def cross(k):
                th, j = divmod(k, XJ)
                rows = FR if j == FB else P
                if j == 0:
                    pe.wait_ge(vec_free, x1_jobs[th])
                if k >= 3:
                    pe.wait_ge(xa_hid, k - 2)
                else:
                    pe.wait_ge(score_done, SCORE_TILES - 3 + k)
                bank = cross_bank(k)[0:rows, :]
                cs = slice(P * j, P * j + rows)
                mm(bank, ctx_T_hi[:, cs], x1_T_hi[th][:, :], start=True, stop=False)
                mm(bank, ctx_T_hi[:, cs], x1_T_lo[th][:, :], start=False, stop=False)
                mm(bank, ctx_T_lo[:, cs], x1_T_hi[th][:, :], start=False, stop=True).then_inc(xa_ready, 1)

            def cross_sum(k):
                th, j = divmod(k, XJ)
                rows = FR if j == FB else P
                if k < XJ and j % 4 == 0:
                    pe.wait_ge(rows_low, j // 4 + 1)
                pe.wait_ge(xa_low[k % 2], k // 2 + 1)
                hi = ctx_hi[0:rows, j, :]
                lo = rest_lo[:, :] if j == FB else ctx_lo[:, j, :]
                mm(acc_banks[th], hi, hid_hi[0:rows, k % 4, :], start=(j == 0), stop=False)
                mm(acc_banks[th], lo, hid_hi[0:rows, k % 4, :], start=False, stop=False)
                mm(acc_banks[th], hi, hid_lo[0:rows, k % 4, :], start=False, stop=(j == FB)).then_inc(xa_summed, 1)

            def weight_transposes(w):
                if w % 4 == 0:
                    pe.wait_ge(experts_here[w // 4], 16)
                if w:
                    pe.wait_ge(wt_taken, w)
                    pe.wait_ge(wt_split, min(w, NE))
                for n in range(4):
                    if w < NE:
                        src = (w13_rows_a, w13_rows_b)[w // 4][:, 4 * (w % 4) + n, :]
                    else:
                        src = w2_rows[:, 2 * (w - NE) + n // 2, P * (n % 2):P * (n % 2 + 1)]
                    last = nc.tensor.transpose(weight_bank[:, P * n:P * (n + 1)], src, ident[:, :])
                last.then_inc(wt_ready, 1)

            def crossed_rows(th):
                slot = vec_slot()
                pe.wait_ge(acc_taken, th + 1)
                for b in range(HB):
                    last = nc.tensor.transpose(slot[:, P * b:P * (b + 1)], acc_T[:, th, P * b:P * (b + 1)], ident[:, :])
                last.then_inc(vec_ready, 1)

            def router_logits(th):
                slot = vec_slot()
                pe.wait_ge(x2_split, th + 1)
                for b in range(HB):
                    last = mm(slot[:, NE * b:NE * (b + 1)], x2_T[:, th, P * b:P * (b + 1)], gate_T[:, :], start=True, stop=True)
                last.then_inc(vec_ready, 1)

            pe.wait_ge(ctx_split, CTX_CHUNKS)
            for k in range(XA + LAG):
                if k < XA:
                    cross(k)
                if k == 0:
                    weighted_sums(STEPS - 1)
                if k == PROJ[1] - 3:
                    attend_rows(UNITS - 1)
                if k == LAG:
                    pe.wait_ge(pv_taken, UNITS)
                if k == PROJ[1]:
                    attended_T(1)
                if k == PROJ[1] + 3:
                    project(1)
                if k == PROJ[1] + 12:
                    rows_to_T(1, 2)
                    x1_jobs.append(jobs[0])
                w = weight_chunk_at(k)
                if w is not None:
                    weight_transposes(w)
                if k == ACC + 3:
                    crossed_rows(0)
                if k == ACC + 12:
                    rows_to_T(0, 3)
                if k == ACC + 17:
                    router_logits(0)
                if k >= LAG:
                    cross_sum(k - LAG)

            def gate_up(u):
                m, ib = divmod(u, 2)
                th, e = divmod(m, NE)
                for n, (ready, read) in enumerate(((gate_ready, moe_silu), (up_ready, moe_act))):
                    if u >= 2:
                        pe.wait_ge(read, u - 1)
                    col = 2 * INTER * e + INTER * n + P * ib
                    hi, lo = w13_T_hi[:, col:col + P], w13_T_lo[:, col:col + P]
                    bank = gate_up_banks[u % 2][:, n, :]
                    mm(bank, hi, x2_T_hi[:, th, :], start=True, stop=False)
                    mm(bank, hi, x2_T_lo[:, th, :], start=False, stop=False)
                    mm(bank, lo, x2_T_hi[:, th, :], start=False, stop=True).then_inc(ready, 1)

            def down(m):
                e = m % NE
                pe.wait_ge(moe_act, 2 * m + 2)
                if m == 1:
                    pe.wait_ge(acc_taken, 2)
                if m >= 2:
                    pe.wait_ge(down_taken, m - 1)
                for b in range(HB):
                    rows = last_banks[b] if m == 2 * NE - 1 else down_banks[m % 2][:, C * b:C * (b + 1)]
                    for ib in range(2):
                        last = mm(rows, act[:, 2 * (m % 2) + ib, P * b:P * (b + 1)],
                                  w2_T[:, (2 * e + ib) * C:(2 * e + ib + 1) * C], start=(ib == 0), stop=(ib == 1))
                    if m == 2 * NE - 1:
                        last.then_inc(down_block, 1)
                if m < 2 * NE - 1:
                    last.then_inc(down_ready, 1)

            pe.wait_ge(wt_split, NE)
            pe.wait_ge(wt_taken, WT_CHUNKS)
            for m in range(2 * NE):
                if m == NE:
                    pe.wait_ge(x2_split, 2)
                gate_up(2 * m)
                gate_up(2 * m + 1)
                if m == 0:
                    crossed_rows(1)
                if m:
                    down(m - 1)
                if m == 3:
                    rows_to_T(1, 4)
                if m == 4:
                    router_logits(1)
            down(2 * NE - 1)

        @block.vector
        def _(ve):
            V = nc.vector
            links, jobs = [0], [0]

            def link(ins):
                links[0] += 1
                ins.then_inc(chain, 1)
                ve.wait_ge(chain, links[0])

            def vec_slot():
                n = jobs[0]
                jobs[0] += 1
                ve.wait_ge(vec_ready, n + 1)
                return pair_of_banks(n)

            link(V.memset(v_strip[:, :, :, :], 0.0))
            V.memset(v_strip[:, :, :, D:D + 1], 1.0).then_inc(strips_set, 1)

            slot = vec_slot()
            V.tensor_copy(x_T[:, 0:HALF], slot[:, 0:HALF]).then_inc(vec_free, 1)

            ve.wait_ge(wqkv_here, 48)
            k_slot, q_slot = vec_slot(), pair_of_banks(2)
            ve.wait_ge(k_made, 1)
            V.scalar_tensor_tensor(out=k_rest[:, :], in0=k_slot, scalar=bias_col[:, 1:2], in1=k_parts[:, 0, :],
                                   op0=ALU.add, op1=ALU.subtract).then_inc(vec_free, 1)

            def q_remains(half):
                hs = halves[half]
                ve.wait_ge(q_made[half], 1)
                return V.scalar_tensor_tensor(out=q_rest[:, hs], in0=q_slot[:, hs], scalar=bias_col[:, 0:1],
                                              in1=q_parts[:, 0, hs], op0=ALU.add, op1=ALU.subtract)

            def q_third(half):
                hs = halves[half]
                ve.wait_ge(q_made[half], 2)
                V.tensor_tensor(q_parts[:, 2, hs], q_rest[:, hs], q_parts[:, 1, hs], ALU.subtract).then_inc(q_made[half], 1)

            vec_slot()
            q_remains(0).then_inc(q_left, 1)
            ve.wait_ge(k_made, 2)
            V.tensor_tensor(k_parts[:, 2, :], k_rest[:, :], k_parts[:, 1, :], ALU.subtract).then_inc(k_made, 1)
            q_third(0)
            q_remains(1).then_inc(vec_free, 1)
            q_third(1)

            slot = vec_slot()
            ve.wait_ge(strips_set, 1)
            for kb in range(KB):
                last = V.tensor_tensor(v_strip[:, kb, :, 0:D], slot[:, C * kb:C * (kb + 1)].rearrange("p (h d) -> p h d", d=D),
                                       bias_v[:, :].rearrange("p (h d) -> p h d", d=D), ALU.add)
            last.then_inc(vec_free, 1)

            def row_max(t):
                slot = vec_slot()
                u, i = divmod(t, UT)
                V.tensor_reduce(neg_max[:, u, i:i + 1], slot, axis=AX.X, op=ALU.max, negate=True).then_inc(vec_free, 1)

            def split_max(u):
                slot = vec_slot()
                src = slot[0:UT, 0:P]
                if u >= 2:
                    ve.wait_ge(m_rows, 16 * PARTS * (u - 1))
                link(V.tensor_copy(m_parts[:, u % 2, 0, :], src))
                V.tensor_tensor(m_rest[:, u % 2, :], src, m_parts[:, u % 2, 0, :], ALU.subtract).then_inc(vec_free, 1)
                ve.wait_ge(vec_free, jobs[0])
                link(V.tensor_copy(m_parts[:, u % 2, 1, :], m_rest[:, u % 2, :]))
                V.tensor_tensor(m_parts[:, u % 2, 2, :], m_rest[:, u % 2, :], m_parts[:, u % 2, 1, :],
                                ALU.subtract).then_inc(m_made, 1)

            def divide(u):
                half, g = divmod(u, NG)
                slot = vec_slot()
                sums = slot[:, 0:HALF].rearrange("p (s w) -> p s w", w=VW)
                V.reciprocal(recip[:, u % 2, :].unsqueeze(2), sums[:, :, D:D + 1]).then_inc(o_read, 1)
                ve.wait_ge(o_read, u + 1)
                dst = att_rows[:, HB * half:HB * (half + 1), GH * D * g:GH * D * (g + 1)]
                over = recip[:, u % 2, :].rearrange("p (b h) -> p b h", h=GH).unsqueeze(3).broadcast_to([P, HB, GH, D])
                V.tensor_tensor(dst.rearrange("p b (h d) -> p b h d", d=D), sums[:, :, 0:D].rearrange("p (b h) d -> p b h d", h=GH),
                                over, ALU.mult).then_inc(vec_free, 1)

            def flat(rows, th):
                return rows[:, HB * th:HB * (th + 1), :].rearrange("p t c -> p (t c)")

            def norm_stats(th):
                for b in range(HB):
                    last = V.bn_stats(stats[:, b, :], pre_norm[:, HB * th + b, :])
                link(last)
                for b in range(HB):
                    last = V.bn_aggr(mean_var[:, b, :], stats[:, b, :])
                link(last)

            def norm_start():
                var, r = norm_s[:, 0, :], norm_s[:, 1, :]
                link(V.tensor_scalar(var, mean_var[:, :, 1], EPS, None, ALU.add))
                link(V.tensor_scalar(r.bitcast(i32), var.bitcast(i32), -0.5, float(0x5F3759DF), ALU.mult, ALU.add))

            def norm_newton():
                var, r, t, t2 = (norm_s[:, i, :] for i in range(4))
                link(V.scalar_tensor_tensor(out=t, in0=r, scalar=-0.5, in1=r, op0=ALU.mult, op1=ALU.mult))
                link(V.tensor_tensor(t2, t, var, ALU.mult))
                link(V.scalar_tensor_tensor(out=r, in0=t2, scalar=1.5, in1=r, op0=ALU.add, op1=ALU.mult))

            def norm_root():
                norm_start()
                for _ in range(NEWTON):
                    norm_newton()

            def norm_apply(th):
                for b in range(HB):
                    tb = HB * th + b
                    last = V.tensor_scalar(x_rows[:, tb, :], pre_norm[:, tb, :], mean_var[:, b, 0:1], norm_s[:, 1, b:b + 1],
                                           ALU.subtract, ALU.mult)
                last.then_inc(normed, 1)

            def take_attended():
                slot = vec_slot()
                V.tensor_copy(att_T[:, :], slot[:, 0:HALF]).then_inc(vec_free, 1)

            def add_projected(th):
                slot = vec_slot()
                ve.wait_ge(pre_bias, 1)
                V.tensor_tensor(flat(pre_norm, th), slot[:, 0:HALF], flat(pre_norm, th), ALU.add).then_inc(vec_free, 1)
                ve.wait_ge(vec_free, jobs[0])

            def high_x1(th):
                slot = vec_slot()
                link(V.tensor_copy(x1_T_hi[th][:, :], slot[:, 0:HALF]))
                return slot

            def low_x1(th, slot):
                V.tensor_tensor(x1_T_lo[th][:, :], slot[:, 0:HALF], x1_T_hi[th][:, :].bitcast(f32), ALU.subtract).then_inc(vec_free, 1)

            for t in range(UT):
                row_max(t)
            split_max(0)
            for t in range(UT, UT + LEAD):
                row_max(t)
            for n in range(STEPS):
                u, kb = divmod(n, KB)
                if kb == 2 and u:
                    divide(u - 1)
                if n == PROJ[0]:
                    take_attended()
                if n == PROJ[0] + 1:
                    add_projected(0)
                    norm_stats(0)
                if n == PROJ[0] + 3:
                    norm_root()
                if n == PROJ[0] + 4:
                    norm_apply(0)
                if n == PROJ[0] + 6:
                    low_x1(0, high_x1(0))
                if kb == KB - 2 and u + 1 < UNITS:
                    split_max(u + 1)
                for t in max_tiles_at(n):
                    row_max(t)

            def add_crossed(th):
                slot = vec_slot()
                V.tensor_tensor(flat(pre_norm, th), slot[:, 0:HALF], flat(x_rows, th), ALU.add).then_inc(vec_free, 1)
                ve.wait_ge(vec_free, jobs[0])

            def take_x2(th):
                slot = vec_slot()
                V.tensor_copy(x2_T[:, th, :], slot[:, 0:HALF]).then_inc(vec_free, 1)
                ve.wait_ge(vec_free, jobs[0])

            def high_x2(th):
                link(V.tensor_copy(x2_T_hi[:, th, :], x2_T[:, th, :]))

            def low_x2(th):
                V.tensor_tensor(x2_T_lo[:, th, :], x2_T[:, th, :], x2_T_hi[:, th, :].bitcast(f32), ALU.subtract).then_inc(x2_split, 1)

            def over_e(a):
                return a.unsqueeze(2).broadcast_to([P, HB, NE])

            sh, ex, sc, masked, sel, wt = (router[:, i, :, :] for i in range(6))
            groups, rank4, rank8 = router[:, 6, :, 0:4], router[:, 6, :, 4:8], router[:, 7, :, :]

            def route_shift():
                slot = vec_slot()
                V.tensor_copy(logits[:, :, :], slot[:, 0:HB * NE].rearrange("p (t e) -> p t e", e=NE)).then_inc(vec_free, 1)
                ve.wait_ge(vec_free, jobs[0])
                link(V.tensor_reduce(small[:, 0, :], logits[:, :, :], axis=AX.X, op=ALU.max))
                V.tensor_tensor(sh, logits[:, :, :], over_e(small[:, 0, :]), ALU.subtract).then_inc(shifted, 1)

            def beats(val, n):
                vi = val.unsqueeze(2).broadcast_to([P, HB, n, n])
                vj = val.unsqueeze(3).broadcast_to([P, HB, n, n])
                V.tensor_tensor(pairs(0, n), vi, vj, ALU.is_gt)
                link(V.tensor_tensor(pairs(1, n), vi, vj, ALU.is_ge))

            def ties(lt, n):
                link(V.tensor_tensor(pairs(1, n), pairs(1, n), lt.unsqueeze(1).broadcast_to([P, HB, n, n]), ALU.mult))
                link(V.tensor_tensor(pairs(0, n), pairs(0, n), pairs(1, n), ALU.max))

            def rank(dst, n):
                link(V.tensor_reduce(dst, pairs(0, n), axis=AX.X, op=ALU.add))

            def pairs(i, n):
                return pair[:, i, 0:HB * n * n].rearrange("p (t j i) -> p t j i", j=n, i=n)

            def route_softmax(th):
                ve.wait_ge(exp_ready, th + 1)
                link(V.tensor_reduce(small[:, 1, :], ex, axis=AX.X, op=ALU.add))
                link(V.reciprocal(small[:, 2, :], small[:, 1, :]))
                link(V.tensor_tensor(sc, ex, over_e(small[:, 2, :]), ALU.mult))

            def route_groups():
                link(V.tensor_tensor(groups, sc[:, :, 0::2], sc[:, :, 1::2], ALU.max))
                ve.wait_ge(masks_made, 2)
                beats(groups, 4)
                ties(lt4[:, :, :], 4)
                rank(rank4, 4)

            def mask_groups():
                link(V.tensor_scalar(groups, rank4, 2.0, None, ALU.is_lt))
                link(V.tensor_tensor(masked.rearrange("p t (g o) -> p t g o", o=2), sc.rearrange("p t (g o) -> p t g o", o=2),
                                     groups.unsqueeze(3).broadcast_to([P, HB, 4, 2]), ALU.mult))

            def route_experts(th):
                link(V.tensor_scalar(sel, rank8, 2.0, None, ALU.is_lt))
                link(V.tensor_tensor(wt, masked, sel, ALU.mult))
                link(V.tensor_reduce(small[:, 3, :], wt, axis=AX.X, op=ALU.add))
                link(V.reciprocal(small[:, 0, :], small[:, 3, :]))
                link(V.tensor_tensor(combine[:, HB * th:HB * (th + 1), :], wt, over_e(small[:, 0, :]), ALU.mult))

            def low(k):
                rows = FR if k % XJ == FB else P
                ve.wait_ge(xa_high, k + 1)
                V.tensor_tensor(hid_lo[0:rows, k % 4, :], hid[0:rows, k % 3, :], hid_hi[0:rows, k % 4, :].bitcast(f32),
                                ALU.subtract).then_inc(xa_low[0], 1)

            def low_weights(e):
                cols = slice(2 * INTER * e, 2 * INTER * (e + 1))
                ve.wait_ge(wt_taken, e + 1)
                V.tensor_tensor(w13_T_lo[:, cols], weight_bank, w13_T_hi[:, cols].bitcast(f32), ALU.subtract).then_inc(wt_split, 1)

            for k in range(XA):
                rows = FR if k % XJ == FB else P
                ve.wait_ge(xa_gelu, k + 1)
                if k >= 3:
                    ve.wait_ge(xa_low[(k - 3) % 2], (k - 3) // 2 + 1)
                V.tensor_tensor(hid[0:rows, k % 3, :], gelu[0:rows, k % 2, :], cross_bank(k)[0:rows, :], ALU.mult).then_inc(xa_hid, 1)
                if k % 2 == 1:
                    low(k - 1)
                w = weight_chunk_at(k - 1)
                if w is not None and w < NE:
                    low_weights(w)
                if k == PROJ[1] - 3:
                    divide(UNITS - 1)
                if k == PROJ[1]:
                    take_attended()
                if k == PROJ[1] + 3:
                    add_projected(1)
                if k == PROJ[1] + 4:
                    norm_stats(1)
                if k == PROJ[1] + 5:
                    norm_start()
                if k in range(PROJ[1] + 6, PROJ[1] + 6 + NEWTON):
                    norm_newton()
                if k == PROJ[1] + 9:
                    norm_apply(1)
                if k == PROJ[1] + 12:
                    slot = high_x1(1)
                if k == PROJ[1] + 13:
                    low_x1(1, slot)
                if k == ACC + 3:
                    add_crossed(0)
                if k == ACC + 4:
                    norm_stats(0)
                if k == ACC + 5:
                    norm_start()
                if k in range(ACC + 6, ACC + 6 + NEWTON):
                    norm_newton()
                if k == ACC + 9:
                    norm_apply(0)
                if k == ACC + 12:
                    take_x2(0)
                if k == ACC + 13:
                    high_x2(0)
                if k == ACC + 14:
                    low_x2(0)
                if k == ACC + 17:
                    route_shift()
                if k == ACC + 20:
                    route_softmax(0)
                if k == ACC + 22:
                    route_groups()
                if k == ACC + 24:
                    mask_groups()
                if k == ACC + 26:
                    beats(masked, NE)
                if k == ACC + 28:
                    ties(lt8[:, :, :], NE)
                if k == ACC + 30:
                    rank(rank8, NE)
                if k == ACC + 31:
                    route_experts(0)

            def hidden(u):
                m, ib = divmod(u, 2)
                ve.wait_ge(moe_silu, u + 1)
                ve.wait_ge(up_ready, u + 1)
                if m >= 2:
                    ve.wait_ge(down_ready, m - 1)
                V.tensor_tensor(act[:, 2 * (m % 2) + ib, :], silu[:, u % 3, :], gate_up_banks[u % 2][:, 1, :],
                                ALU.mult).then_inc(moe_act, 1)

            def add_expert(m):
                th, e = divmod(m, NE)
                ve.wait_ge(down_ready, m + 1)
                if e:
                    ve.wait_ge(down_taken, m)
                for b in range(HB):
                    tb = HB * th + b
                    base = pre_norm if e else x_rows
                    last = V.scalar_tensor_tensor(out=pre_norm[:, tb, :], in0=down_banks[m % 2][:, C * b:C * (b + 1)],
                                                  scalar=combine[:, tb, e:e + 1], in1=base[:, tb, :], op0=ALU.mult, op1=ALU.add)
                last.then_inc(down_taken, 1)

            for m in range(2 * NE):
                hidden(2 * m)
                hidden(2 * m + 1)
                if m == 0:
                    add_crossed(1)
                    norm_stats(1)
                if m:
                    add_expert(m - 1)
                if m == 1:
                    norm_root()
                if m == 2:
                    norm_apply(1)
                if m == 3:
                    take_x2(1)
                    high_x2(1)
                    low_x2(1)
                if m == 4:
                    route_shift()
                if m == 6:
                    route_softmax(1)
                    route_groups()
                    mask_groups()
                if m == 7:
                    beats(masked, NE)
                    ties(lt8[:, :, :], NE)
                    rank(rank8, NE)
                    route_experts(1)
                if m == NE + 1:
                    ve.wait_ge(down_taken, NE)
                    norm_stats(0)
                if m == NE + 2:
                    norm_root()
                if m == NE + 3:
                    norm_apply(0)
            ve.wait_ge(down_taken, 2 * NE - 1)
            for b in range(HB):
                tb = HB + b
                ve.wait_ge(down_block, b + 1)
                V.scalar_tensor_tensor(out=pre_norm[:, tb, :], in0=last_banks[b],
                                       scalar=combine[:, tb, NE - 1:NE], in1=pre_norm[:, tb, :], op0=ALU.mult,
                                       op1=ALU.add).then_inc(last_sum, 1)
                ve.wait_ge(last_sum, b + 1)
                last = V.bn_stats(stats[:, b, :], pre_norm[:, tb, :])
            link(last)
            for b in range(HB):
                last = V.bn_aggr(mean_var[:, b, :], stats[:, b, :])
            link(last)
            norm_root()
            norm_apply(1)


_INS = ['x', 'ctx_1024', 'L0_attn_qkv_w', 'L0_attn_qkv_b', 'L0_attn_proj_w', 'L0_attn_proj_b', 'L0_ffn_gate_w',
        'L0_ffn_w13_weight', 'L0_ffn_w2_weight']


def kernel(**inputs):
    import numpy as _np
    import concourse.bacc as _bacc
    from concourse import mybir as _mybir
    from concourse.bass_utils import run_bass_kernel_spmd as _run

    nc = _bacc.Bacc("TRN2", target_bir_lowering=False, num_devices=1)
    arrays, args = {}, []
    for name in _INS:
        a = _np.ascontiguousarray(inputs[name])
        arrays[f"in_{name}"] = a
        args.append(nc.dram_tensor(f"in_{name}", a.shape, _mybir.dt.from_np(a.dtype), kind="ExternalInput").ap())
    args.append(nc.dram_tensor("out_0", (1, N, C), _mybir.dt.float32, kind="ExternalOutput").ap())
    args.append(nc.dram_tensor("kept_k", (PARTS, D, H, N), _mybir.dt.bfloat16, kind="Internal").ap())
    args.append(nc.dram_tensor("kept_q", (2, PARTS, D, H, HALF), _mybir.dt.bfloat16, kind="Internal").ap())
    build(nc, *args)
    r = _run(nc, [arrays], core_ids=[0])
    return r.results[0]["out_0"]
```
